# Optimizing a Trainium2 kernel written in Bass

```python
import numpy as np
import jax
import jax.numpy as jnp

def _softmax(x, axis=-1):
    return jax.nn.softmax(x, axis=axis)

def _gelu(x):
    return jax.nn.gelu(x, approximate=True)

def _silu(x):
    return jax.nn.silu(x)

def _sigmoid(x):
    return jax.nn.sigmoid(x)

def _layernorm(x, axis=-1, eps=1e-05):
    m = jnp.mean(x, axis=axis, keepdims=True)
    v = jnp.var(x, axis=axis, keepdims=True)
    return (x - m) / jnp.sqrt(v + eps)

def _scatter_add(tgt, idx, src, axis=0):
    return tgt.at[idx].add(src)

def _segment_sum(src, seg, n):
    return jax.ops.segment_sum(src, seg, n)
kernel_name = 'mk_adaln_d1_jaxref_r4_b24731'

def setup_inputs(seed: int=0):
    np.random.seed(seed)
    _w = jnp.asarray

    def _L0_attn_setup():
        import jax, jax.numpy as jnp
        import numpy as np
        HID = 256
        NH = 16
        HD = HID // NH
        RANK = 16
        B, L = (2, 512)
        key = jax.random.key(seed)
        ks = jax.random.split(key, 9)
        s = 0.02
        return {'x': jax.random.normal(ks[0], (B, L, HID), dtype=jnp.float32), 'Wq': jax.random.normal(ks[1], (HID, HID), dtype=jnp.float32) * s, 'Wk': jax.random.normal(ks[2], (HID, HID), dtype=jnp.float32) * s, 'Wv': jax.random.normal(ks[3], (HID, HID), dtype=jnp.float32) * s, 'Wg': jax.random.normal(ks[4], (HID, HID), dtype=jnp.float32) * s, 'Wgk1': jax.random.normal(ks[5], (HID, RANK), dtype=jnp.float32) * s, 'Wgk2': jax.random.normal(ks[6], (RANK, HID), dtype=jnp.float32) * s, 'bgk2': jnp.zeros((HID,), dtype=jnp.float32), 'gamma': jnp.ones((HID,), dtype=jnp.float32), 'beta': jnp.zeros((HID,), dtype=jnp.float32), 'Wout': jax.random.normal(ks[7], (HID, HID), dtype=jnp.float32) * s}
    _L0_attn_in = _L0_attn_setup()

    def _L0_ffn_setup():
        import jax, jax.numpy as jnp
        import numpy as np
        E = 8
        K = 2
        D = 256
        P = 1024
        key = jax.random.key(seed)
        ks = jax.random.split(key, 8)
        s = lambda fan_in: 1.0 / np.sqrt(fan_in)
        x = jax.random.normal(ks[0], (2, 512, D), dtype=jnp.float32)
        W1 = jax.random.normal(ks[1], (E, D, P), dtype=jnp.float32) * s(D)
        b1 = jax.random.normal(ks[2], (E, P), dtype=jnp.float32) * 0.01
        W2 = jax.random.normal(ks[3], (E, P, D), dtype=jnp.float32) * s(P)
        b2 = jax.random.normal(ks[4], (E, D), dtype=jnp.float32) * 0.01
        Wr = jax.random.normal(ks[5], (D, E), dtype=jnp.float32) * s(D)
        br = jax.random.normal(ks[6], (E,), dtype=jnp.float32) * 0.01
        return {'x': x, 'W1': W1, 'b1': b1, 'W2': W2, 'b2': b2, 'Wr': Wr, 'br': br}
    _L0_ffn_in = _L0_ffn_setup()
    _L0_c = _w((lambda *s: np.random.randn(*s).astype(np.float32) * 0.05)(1, 256))
    _L0_wmod = _w((lambda *s: np.random.randn(*s).astype(np.float32) * 0.05)(256, 6 * 256) * 256 ** (-0.5))
    _d = {'L0_attn_x': _L0_attn_in['x'], 'L0_attn_Wq': _L0_attn_in['Wq'], 'L0_attn_Wk': _L0_attn_in['Wk'], 'L0_attn_Wv': _L0_attn_in['Wv'], 'L0_attn_Wg': _L0_attn_in['Wg'], 'L0_attn_Wgk1': _L0_attn_in['Wgk1'], 'L0_attn_Wgk2': _L0_attn_in['Wgk2'], 'L0_attn_bgk2': _L0_attn_in['bgk2'], 'L0_attn_gamma': _L0_attn_in['gamma'], 'L0_attn_beta': _L0_attn_in['beta'], 'L0_attn_Wout': _L0_attn_in['Wout'], 'L0_ffn_W1': _L0_ffn_in['W1'], 'L0_ffn_b1': _L0_ffn_in['b1'], 'L0_ffn_W2': _L0_ffn_in['W2'], 'L0_ffn_b2': _L0_ffn_in['b2'], 'L0_ffn_Wr': _L0_ffn_in['Wr'], 'L0_ffn_br': _L0_ffn_in['br'], 'L0_c': _L0_c, 'L0_wmod': _L0_wmod}
    _x0 = _d['L0_attn_x']
    _d['L0_attn_x'] = jax.random.normal(jax.random.fold_in(jax.random.key(seed), 1), (1, 4096, 256), dtype=_x0.dtype)
    del _x0
    return _d

def reference(L0_attn_x, L0_attn_Wq, L0_attn_Wk, L0_attn_Wv, L0_attn_Wg, L0_attn_Wgk1, L0_attn_Wgk2, L0_attn_bgk2, L0_attn_gamma, L0_attn_beta, L0_attn_Wout, L0_ffn_W1, L0_ffn_b1, L0_ffn_W2, L0_ffn_b2, L0_ffn_Wr, L0_ffn_br, L0_c, L0_wmod):

    def _L0_attn_ref(x, Wq, Wk, Wv, Wg, Wgk1, Wgk2, bgk2, gamma, beta, Wout):
        import jax, jax.numpy as jnp
        import numpy as np
        HID = 256
        NH = 16
        HD = HID // NH
        RANK = 16
        B, L = (2, 512)
        Bb, Ll, Hid = x.shape
        H, Dh = (NH, HD)
        q = (x @ Wq).reshape(Bb, Ll, H, Dh)
        k = (x @ Wk).reshape(Bb, Ll, H, Dh)
        v = (x @ Wv).reshape(Bb, Ll, H, Dh)
        gk = (jax.nn.log_sigmoid(x @ Wgk1 @ Wgk2 + bgk2) / 16.0).reshape(Bb, Ll, H, Dh)
        qT = jnp.transpose(q, (1, 0, 2, 3))
        kT = jnp.transpose(k, (1, 0, 2, 3))
        vT = jnp.transpose(v, (1, 0, 2, 3))
        gT = jnp.transpose(gk, (1, 0, 2, 3))

        def step(state, inp):
            qt, kt, vt, gt = inp
            gate = jnp.exp(gt)
            state = state * gate[..., None] + vt[..., None] * kt[..., None, :]
            out_t = jnp.einsum('bhvk,bhk->bhv', state, qt)
            return (state, out_t)
        state0 = jnp.zeros((Bb, H, Dh, Dh), dtype=x.dtype)
        _, outs = jax.lax.scan(step, state0, (qT, kT, vT, gT))
        out = jnp.transpose(outs, (1, 0, 2, 3)).reshape(Bb, Ll, Hid)
        mu = out.mean(-1, keepdims=True)
        var = out.var(-1, keepdims=True)
        out = (out - mu) / jnp.sqrt(var + 1e-05) * gamma + beta
        out = out * jax.nn.silu(x @ Wg)
        return out @ Wout

    def _L0_ffn_ref(x, W1, b1, W2, b2, Wr, br):
        import jax, jax.numpy as jnp
        import numpy as np
        E = 8
        K = 2
        D = 256
        P = 1024
        B, S, _ = x.shape
        xf = x.reshape(B * S, D)
        scores = xf @ Wr + br
        _, top_idx = jax.lax.top_k(scores, K)
        mask = jax.nn.one_hot(top_idx, E, dtype=scores.dtype).sum(-2) > 0
        router_weights = jax.nn.softmax(jnp.where(mask, scores, -jnp.inf), axis=-1)
        h = jax.nn.gelu(jnp.einsum('td,edp->etp', xf, W1) + b1[:, None, :])
        y = jnp.einsum('etp,epd->etd', h, W2) + b2[:, None, :]
        out = jnp.einsum('te,etd->td', router_weights, y)
        return out.reshape(B, S, D)
    x = L0_attn_x
    mod = (_silu(L0_c) @ L0_wmod).reshape(L0_c.shape[0], 6, 1, -1)
    sa, ca, ga, sb, cb, gb = (mod[:, 0], mod[:, 1], mod[:, 2], mod[:, 3], mod[:, 4], mod[:, 5])
    ga = (2 * (ga >= 0) - 1) * jnp.maximum(jnp.abs(ga), 0.25)
    gb = (2 * (gb >= 0) - 1) * jnp.maximum(jnp.abs(gb), 0.25)
    h = _layernorm(x, axis=-1) * (1 + ca) + sa
    x = x + ga * _L0_attn_ref(h, L0_attn_Wq, L0_attn_Wk, L0_attn_Wv, L0_attn_Wg, L0_attn_Wgk1, L0_attn_Wgk2, L0_attn_bgk2, L0_attn_gamma, L0_attn_beta, L0_attn_Wout)
    h = _layernorm(x, axis=-1) * (1 + cb) + sb
    x = x + gb * _L0_ffn_ref(h, L0_ffn_W1, L0_ffn_b1, L0_ffn_W2, L0_ffn_b2, L0_ffn_Wr, L0_ffn_br)
    return x

_drawn_inputs = setup_inputs


def setup_inputs(seed=0):
    import zlib

    import numpy as np

    out = dict(_drawn_inputs(seed))
    spreads = {'L0_attn_bgk2': (0.0, 0.8), 'L0_attn_gamma': (1.0, 0.6), 'L0_attn_beta': (0.0, 0.8)}
    factors = {'L0_attn_Wq': 3.406,
     'L0_attn_Wk': 3.474,
     'L0_attn_Wv': 3.461,
     'L0_attn_Wg': 3.492,
     'L0_attn_Wgk1': 8.0,
     'L0_attn_Wgk2': 8.0,
     'L0_attn_Wout': 3.427,
     'L0_ffn_b1': 47.507,
     'L0_ffn_b2': 31.977,
     'L0_ffn_br': 6.578}
    for name, (base, spread) in spreads.items():
        noise = np.random.default_rng([zlib.crc32(name.encode()), seed]).standard_normal(out[name].shape)
        drawn = base * np.exp(spread * noise) if base else spread * noise
        out[name] = jnp.asarray(drawn.astype(out[name].dtype))
    for name, factor in factors.items():
        out[name] = (out[name] * factor).astype(out[name].dtype)
    return out
```

```python
from contextlib import ExitStack

import concourse.bass as bass
from concourse import mybir

F32 = mybir.dt.float32
I32 = mybir.dt.int32
U32 = mybir.dt.uint32
ALU = mybir.AluOpType
ACT = mybir.ActivationFunctionType
AX_X = mybir.AxisListType.X

P = 128
EPS = 1e-5
GATE_DIVISOR = 16.0
MIN_GATE = 0.25


def build(nc, x, Wq, Wk, Wv, Wg, Wgk1, Wgk2, bgk2, gamma, beta, Wout, W1, b1, W2, b2, Wr, br, cond, wmod, out):
    _, T, D = x.shape
    E, _, FF = W1.shape
    RANK = Wgk1.shape[1]
    KD = D // P
    KF = FF // P
    HD = 16
    HB = P // HD
    NC = T // P
    TOP = 2
    REGION = T + P
    TILES = TOP * T // P + E
    ROW = D + 16
    ID = D + E
    VSTEP = HB * HD + HD
    assert KD == 2 and NC % 2 == 0 and TILES % 2 == 0 and D == 256

    xt = x.rearrange("b t d -> (b t) d")
    scratch = nc.dram_tensor("expert_rows", (E * REGION + E * P, ROW), F32, kind="Internal").ap()

    with ExitStack() as ctx:
        def sb(name, shape, dt=F32):
            return ctx.enter_context(nc.sbuf_tensor(name, shape, dt))

        def sem(name):
            return ctx.enter_context(nc.semaphore(name))

        def bank(name):
            return ctx.enter_context(nc.psum_tensor(name, [P, 512], F32))

        p_tr = bank("p_tr")
        p_qk = bank("p_qk")
        p_vg = bank("p_vg")
        p_z = bank("p_z")
        p_cum = bank("p_cum")
        p_a = [bank("p_a0"), bank("p_a1")]
        p_o = bank("p_o")

        w1 = sb("w1", [P, E * KD * FF])
        w2 = sb("w2", [P, E * KF * D])
        wqk = sb("wqk", [P, KD, 2 * D])
        wvg = sb("wvg", [P, KD, 2 * D])
        wout = sb("wout", [P, KD, D])
        wgk1 = sb("wgk1", [P, KD, RANK])
        wgk2 = sb("wgk2", [RANK + 1, D])
        wr = sb("wr", [P, KD, E])
        gam = sb("gam", [P, D])
        bet = sb("bet", [P, D])
        br_all = sb("br_all", [P, E])
        b2_all = sb("b2_all", [P, E * D])
        b1_rows = sb("b1_rows", [E * KF, P])
        b1_col = sb("b1_col", [P, E * KF])
        ident = sb("ident", [P, P])
        upto = sb("upto", [P, P])
        before = sb("before", [P, P])
        ones = sb("ones", [P, P])
        own = sb("own", [P, HB])
        eps = sb("eps", [P, 1])
        iota_e = sb("iota_e", [P, E])
        region0 = sb("region0", [P, E])
        ids = sb("ids", [P, NC + 1])
        cnd = sb("cnd", [P, KD])
        cnd_e = sb("cnd_e", [P, KD])
        cnd_s = sb("cnd_s", [P, KD])
        cnd_all = sb("cnd_all", [P, KD, P])
        mods = sb("mods", [P, 8])
        ga = sb("ga", [P, D])
        gb = sb("gb", [P, D])
        tmp_g = sb("tmp_g", [P, D])
        pad_rows = sb("pad_rows", [P, ROW])

        class Lodger:
            def __init__(self, host, start):
                self.host, self.at = host, start

            def take(self, *dims):
                n = 1
                for d in dims:
                    n *= d
                self.at += n
                assert self.at <= self.host.shape[1]
                return self.host[:, self.at - n:self.at]

        LATE = 2
        wm = w2[:, (E - LATE) * KF * D:(E - LATE) * KF * D + KD * 6 * D].rearrange("p (j n) -> p j n", j=KD)
        in_w1, in_w2 = Lodger(w1, (E - LATE) * KD * FF), Lodger(w2, (E - LATE) * KF * D)

        x_in = [sb(f"x_in{i}", [P, D]) for i in range(2)]
        x_res = [sb(f"x_res{i}", [P, D]) for i in range(2)]
        xn = [sb(f"xn{i}", [P, D]) for i in range(2)]
        st_x = sb("st_x", [P, 6])
        mv_x = sb("mv_x", [P, 4])
        hT = sb("hT", [P, KD, P])
        rT = sb("rT", [RANK + 1, P])
        qbd = in_w2.take(KD, HB, P).rearrange("p (a h t) -> p a h t", a=KD, h=HB)
        qk = [in_w2.take(2 * D) for i in range(2)]
        qkT = [sb(f"qkT{i}", [P, 2 * KD, P]) for i in range(2)]
        vbd = in_w1.take(KD, HB * VSTEP).rearrange("p (a c) -> p a c", a=KD)
        vn = [in_w1.take(D) for i in range(2)]
        abs_z = in_w1.take(D)
        ez = in_w1.take(D)
        lz = in_w2.take(D)
        eg = sb("eg", [P, D])
        silu = in_w1.take(D)
        g_log = in_w2.take(D)
        e_pos = [sb(f"e_pos{i}", [P, D]) for i in range(2)]
        e_neg = in_w2.take(D)
        e_tot = in_w2.take(D)
        decay = [in_w1.take(D) for i in range(2)]
        w_ln = [sb(f"w_ln{i}", [P, D]) for i in range(2)]
        b_ln = [sb(f"b_ln{i}", [P, D]) for i in range(2)]
        am = sb("am", [P, 4, 512])
        oT = sb("oT", [P, D])
        o_tok = sb("o_tok", [P, D])
        st_o = sb("st_o", [P, 6])
        mv_o = sb("mv_o", [P, 4])
        o_ln = sb("o_ln", [P, D])
        o_ln2 = sb("o_ln2", [P, D])
        owT = sb("owT", [P, D])
        state = sb("state", [P, D])
        state_sum = sb("state_sum", [P, D])
        x1 = [sb(f"x1{i}", [P, D]) for i in range(2)]
        st_1 = sb("st_1", [P, 6])
        mv_1 = sb("mv_1", [P, 4])
        rows = [sb(f"rows{i}", [P, ROW]) for i in range(2)]
        h2T = sb("h2T", [P, KD, P])
        score = sb("score", [P, E])
        top = sb("top", [P, 8])
        top_i = sb("top_i", [P, 8], U32)
        top_f = sb("top_f", [P, TOP])
        hot = [sb(f"hot{j}", [P, E]) for j in range(TOP)]
        chosen = sb("chosen", [P, E])
        gap = sb("gap", [P, 1])
        gap_e = sb("gap_e", [P, 1])
        wt = sb("wt", [P, 3])
        wt_a = sb("wt_a", [P, E])
        base = sb("base", [P, E])
        slot = sb("slot", [P, E])
        pick = sb("pick", [P, E])
        pos_f = sb("pos_f", [P, TOP])
        pos = [sb(f"pos{i}", [P, TOP], U32) for i in range(2)]

        n_rows = sb("n_rows", [P, E])
        it32 = sb("it32", [P, NC])
        over = am[:, 0, 0:E * NC].rearrange("p (e n) -> p e n", e=E)
        n_tiles = sb("n_tiles", [P, E])
        one_e = sb("one_e", [P, E])
        ends = sb("ends", [P, E])
        it72 = sb("it72", [P, TILES])
        past = am[:, 1:3, :].rearrange("p a b -> p (a b)")[:, 0:TILES * E].rearrange("p (i e) -> p i e", e=E)
        past_n = sb("past_n", [P, TILES, E])[:]
        tile_e = sb("tile_e", [P, TILES])
        tile_s = sb("tile_s", [P, TILES])
        tile_r = sb("tile_r", [P, TILES])
        tab_e = sb("tab_e", [P, TILES], I32)
        tab_r = sb("tab_r", [P, TILES], I32)
        tab_p = sb("tab_p", [P, E], I32)
        xs = [sb(f"xs{i}", [P, ROW]) for i in range(3)][:2]
        xsT = h2T
        hid = am[:, 0:2, :].rearrange("p a b -> p (a b)")
        act = am[:, 2:4, :].rearrange("p a b -> p (a b)")
        y_b = o_tok
        y_out = x1
        tok = [sb(f"tok{i}", [P, 1], U32) for i in range(2)]

        small_loaded = sem("small_loaded")
        attn_w_loaded = sem("attn_w_loaded")
        experts_loaded = sem("experts_loaded")
        consts_made = sem("consts_made")
        pool_made = sem("pool_made")
        cond_exp = sem("cond_exp")
        cond_spread = sem("cond_spread")
        mod_ready = sem("mod_ready")
        mods_taken = sem("mods_taken")
        xin_loaded = [sem(f"xin_loaded{i}") for i in range(2)]
        xres_loaded = [sem(f"xres_loaded{i}") for i in range(2)]
        x1_stored = [sem(f"x1_stored{i}") for i in range(2)]
        rows_sent = [sem(f"rows_sent{i}") for i in range(2)]
        dve_ln = sem("dve_ln")
        dve_f = sem("dve_f")
        dve_b = sem("dve_b")
        dve_r = sem("dve_r")
        dve_s = sem("dve_s")
        act_f = sem("act_f")
        act_x = sem("act_x")
        act_o = sem("act_o")
        act_1 = sem("act_1")
        x_stats, x_scale = sem("x_stats"), sem("x_scale")
        o_stats, o_scale = sem("o_stats"), sem("o_scale")
        x1_stats, x1_scale = sem("x1_stats"), sem("x1_scale")
        xn_ready = sem("xn_ready")
        xT_ready = sem("xT_ready")
        hT_ready = sem("hT_ready")
        proj_ready = sem("proj_ready")
        qk_taken = sem("qk_taken")
        gate_exp = sem("gate_exp")
        silu_ready = sem("silu_ready")
        ln_scales_ready = sem("ln_scales_ready")
        r_ready = sem("r_ready")
        rT_ready = sem("rT_ready")
        z_ready = sem("z_ready")
        log1p_ready = sem("log1p_ready")
        g_ready = sem("g_ready")
        cum_ready = sem("cum_ready")
        e_ready = sem("e_ready")
        decay_ready = sem("decay_ready")
        vn_ready = sem("vn_ready")
        vbd_ready = sem("vbd_ready")
        qkT_ready = sem("qkT_ready")
        qkT_taken = sem("qkT_taken")
        qbd_ready = sem("qbd_ready")
        a_ready = sem("a_ready")
        am_ready = sem("am_ready")
        o_ready = sem("o_ready")
        oT_taken = sem("oT_taken")
        u_ready = sem("u_ready")
        state_ready = sem("state_ready")
        ot_ready = sem("ot_ready")
        o_ln_ready = sem("o_ln_ready")
        owT_ready = sem("owT_ready")
        owT_taken = sem("owT_taken")
        y_ready = sem("y_ready")
        x1_ready = sem("x1_ready")
        xn2_ready = sem("xn2_ready")
        x2T_ready = sem("x2T_ready")
        h2T_ready = sem("h2T_ready")
        score_ready = sem("score_ready")
        gap_ready = sem("gap_ready")
        gap_exp = sem("gap_exp")
        chosen_ready = sem("chosen_ready")
        rank_ready = sem("rank_ready")
        pos_ready = sem("pos_ready")
        id_ready = sem("id_ready")
        pads_stored = sem("pads_stored")
        tables_ready = sem("tables_ready")
        xs_loaded = [sem(f"xs_loaded{i}") for i in range(2)]
        m_xT = sem("m_xT")
        m_xT_taken = sem("m_xT_taken")
        m_hid = sem("m_hid")
        m_hid_taken = sem("m_hid_taken")
        m_hidT = sem("m_hidT")
        m_act = sem("m_act")
        m_y = sem("m_y")
        m_y_biased = sem("m_y_biased")
        m_out = sem("m_out")
        m_tok = sem("m_tok")
        added = [sem(f"added{i}") for i in range(2)]

        block = ctx.enter_context(nc.Block())

        class Order:

            def __init__(self, eng, sm):
                self.eng, self.sm, self.start, self.n, self.per = eng, sm, 0, 0, None

            def begin(self, c):
                if self.n and self.per is None:
                    self.per = self.n
                assert self.n in (0, self.per)
                self.start = 0 if self.per is None else c * self.per
                self.n = 0

            def then(self, ins, apart=False):
                self.n += 1
                ins.then_inc(self.sm, 1)
                if apart:
                    wait_apart(self.eng, (self.sm, self.start + self.n))
                else:
                    self.eng.wait_ge(self.sm, self.start + self.n)

        def wait_apart(eng, *waits):
            waits = [(sm, v if isinstance(v, int) else eng.to_reg(v)) for sm, v in waits]
            eng.wait_ge(consts_made, 1)
            for sm, v in waits:
                eng.wait_ge(sm, v)

        def after(eng, sm, value):
            if not isinstance(value, int) or value > 0:
                eng.wait_ge(sm, value)

        def walk(eng, step):
            step(-1, 1, True, False, False)
            step(0, 0, True, True, False)
            step(1, 1, True, True, True)
            with eng.Fori(1, NC // 2 - 1) as i:
                step(2 * i, 0, True, True, True)
                step(2 * i + 1, 1, True, True, True)
            step(NC - 2, 0, True, True, True)
            step(NC - 1, 1, False, True, True)
            step(NC, 0, False, False, True)

        def walk_tiles(eng, step):
            step(-1, 1, True, False)
            step(0, 0, True, True)
            step(1, 1, True, True)
            with eng.Fori(1, TILES // 2 - 1) as i:
                step(2 * i, 0, True, True)
                step(2 * i + 1, 1, True, True)
            step(TILES - 2, 0, True, True)
            step(TILES - 1, 1, False, True)

        @block.sync
        def _(sp):
            def load(dst, src, sm):
                sp.dma_start(dst, src).then_inc(sm, 16)

            load(x_in[0][:], xt[0:P, :], xin_loaded[0])
            load(x_in[1][:], xt[P:2 * P, :], xin_loaded[1])
            with nc.allow_non_contiguous_dma(reason="256 numbers"):
                load(cnd[:], cond.rearrange("a (j p) -> p (a j)", p=P), small_loaded)
            load(wm, wmod.rearrange("(j p) n -> p j n", p=P), small_loaded)
            load(gam[:], gamma.rearrange("(a d) -> a d", a=1).to_broadcast([P, D]), small_loaded)
            load(bet[:], beta.rearrange("(a d) -> a d", a=1).to_broadcast([P, D]), small_loaded)
            load(br_all[:], br.rearrange("(a d) -> a d", a=1).to_broadcast([P, E]), small_loaded)
            load(b2_all[:], b2.rearrange("(a e) d -> a (e d)", a=1).to_broadcast([P, E * D]), small_loaded)
            load(b1_rows[:], b1.rearrange("e (j p) -> (e j) p", p=P), small_loaded)
            for k, w in enumerate((Wq, Wk)):
                load(wqk[:, :, k * D:(k + 1) * D], w.rearrange("(j p) n -> p j n", p=P), attn_w_loaded)
            for k, w in enumerate((Wv, Wg)):
                load(wvg[:, :, k * D:(k + 1) * D], w.rearrange("(j p) n -> p j n", p=P), attn_w_loaded)
            load(wout[:], Wout.rearrange("(j p) n -> p j n", p=P), attn_w_loaded)
            load(wgk1[:], Wgk1.rearrange("(j p) n -> p j n", p=P), attn_w_loaded)
            load(wgk2[0:RANK, :], Wgk2, attn_w_loaded)
            load(wgk2[RANK:RANK + 1, :], bgk2.rearrange("(a d) -> a d", a=1), attn_w_loaded)
            load(wr[:], Wr.rearrange("(j p) n -> p j n", p=P), attn_w_loaded)

            sp.wait_ge(consts_made, 1)
            for k in range(E):
                load(scratch[E * REGION + k * P:E * REGION + (k + 1) * P, :], pad_rows[:], pads_stored)
            load(out[T:T + P, :], pad_rows[:, 0:D], pads_stored)

            def expert(e):
                load(w1[:, e * KD * FF:(e + 1) * KD * FF].rearrange("p (j n) -> p j n", j=KD),
                     W1[e].rearrange("(j p) n -> p j n", p=P), experts_loaded)
                load(w2[:, e * KF * D:(e + 1) * KF * D].rearrange("p (j n) -> p j n", j=KF),
                     W2[e].rearrange("(j p) n -> p j n", p=P), experts_loaded)

            def step(c, u, front, back, route):
                if back and not (isinstance(c, int) and c + 2 >= NC):
                    sp.wait_ge(xn_ready, c + 1)
                    load(x_in[u][:], xt[bass.ds((c + 2) * P, P), :], xin_loaded[u])
                if front:
                    after(sp, x1_ready, c)
                    load(x_res[1 - u][:], xt[bass.ds((c + 1) * P, P), :], xres_loaded[1 - u])
                if back:
                    sp.wait_ge(x1_ready, c + 1)
                    load(out[bass.ds(c * P, P), :], x1[u][:], x1_stored[u])
                if isinstance(c, int) and c == 0:
                    sp.wait_ge(mod_ready, 1)
                    for e in range(E - LATE):
                        expert(e)

            walk(sp, step)

            sp.wait_ge(tables_ready, 1)
            for e in range(E - LATE, E):
                expert(e)

            for e in range(E):
                first = sp.value_load(tab_p[0:1, e:e + 1], min_val=e * REGION, max_val=e * REGION + T)
                load(scratch[bass.ds(first, P), :], pad_rows[:], pads_stored)
            sp.wait_ge(pads_stored, 16 * (2 * E + 1))
            for u in range(2):
                sp.wait_ge(rows_sent[u], 16 * TOP * NC // 2)

            def rows_of(i, u):
                first = sp.value_load(tab_r[0:1, bass.ds(i, 1)], min_val=0, max_val=E * REGION + (E - 1) * P)
                after(sp, m_out, i - 1)
                load(xs[u][:], scratch[bass.ds(first, P), :], xs_loaded[u])

            def tile_step(i, u, ahead, here):
                if ahead:
                    rows_of(i + 1, 1 - u)

            walk_tiles(sp, tile_step)
            for u in range(2):
                sp.wait_ge(x1_stored[u], 16 * NC // 2)
                sp.wait_ge(added[u], 16 * TILES // 2)

        @block.gpsimd
        def _(pool):
            order = Order(pool, pool_made)
            order.then(nc.gpsimd.memset(ident[:], 0.0))
            order.then(nc.gpsimd.affine_select(out=ident[:], in_=ident[:], compare_op=ALU.not_equal, fill=1.0,
                                               base=0, pattern=[[-1, P]], channel_multiplier=1))
            order.then(nc.gpsimd.memset(ones[:], 1.0))
            nc.gpsimd.affine_select(out=upto[:], in_=ones[:], compare_op=ALU.is_ge, fill=0.0,
                                    base=0, pattern=[[1, P]], channel_multiplier=-1)
            nc.gpsimd.affine_select(out=before[:], in_=ones[:], compare_op=ALU.is_ge, fill=0.0,
                                    base=-1, pattern=[[1, P]], channel_multiplier=-1)
            order.then(nc.gpsimd.affine_select(out=own[:], in_=ones[:, 0:HB], compare_op=ALU.is_ge, fill=0.0,
                                               base=0, pattern=[[-HD, HB]], channel_multiplier=1))
            nc.gpsimd.affine_select(out=own[:], in_=own[:], compare_op=ALU.is_ge, fill=0.0,
                                    base=HD - 1, pattern=[[HD, HB]], channel_multiplier=-1)

            def numbers(dst, pattern, by_partition):
                nc.gpsimd.iota(dst, pattern=pattern, base=0, channel_multiplier=by_partition,
                               allow_small_or_imprecise_dtypes=True)

            numbers(iota_e[:], [[1, E]], 0)
            numbers(region0[:], [[REGION, E]], 0)
            numbers(base[:], [[REGION, E]], 0)
            numbers(ids[:], [[P, NC + 1]], 1)
            numbers(it32[:], [[P, NC]], 0)
            numbers(it72[:], [[1, TILES]], 0)
            order.then(nc.gpsimd.memset(pad_rows[:], 0.0))
            order.then(nc.gpsimd.tensor_copy(pad_rows[:, ID:ID + 1], ids[:, NC:NC + 1]))
            nc.gpsimd.memset(one_e[:], 1.0)
            nc.gpsimd.memset(eps[:], EPS)
            nc.gpsimd.memset(state[:], 0.0)
            for r in rows:
                nc.gpsimd.memset(r[:], 0.0)
            nc.gpsimd.memset(rT[:], 1.0)
            nc.gpsimd.memset(vbd[:], 0.0).then_inc(consts_made, 1)
            pool.wait_ge(consts_made, 1)

            def step(c, u, front, back, route):
                f, v = c + 1, 1 - u
                if front:
                    pool.wait_ge(silu_ready, f + 1)
                    after(pool, o_ln_ready, f - 1)
                    nc.gpsimd.tensor_tensor(w_ln[v][:], silu[:], gam[:], ALU.mult)
                    nc.gpsimd.tensor_tensor(b_ln[v][:], silu[:], bet[:], ALU.mult).then_inc(ln_scales_ready, 1)
                if route:
                    wait_apart(pool, (xn2_ready, c))
                    nc.gpsimd.tensor_copy(rows[1 - u][:, ID:ID + 1], ids[:, bass.ds(c - 1, 1)]).then_inc(id_ready, 1)
                    wait_apart(pool, (id_ready, c), (pos_ready, c))
                    for j in range(TOP):
                        nc.gpsimd.indirect_dma_start(
                            out=scratch, out_offset=bass.IndirectOffsetOnAxis(ap=pos[1 - u][:, j:j + 1], axis=0),
                            in_=rows[1 - u][:], in_offset=None,
                        ).then_inc(rows_sent[1 - u], 16)
                if front:
                    pool.wait_ge(e_ready, f + 1)
                    after(pool, state_ready, f - 1)
                    for j in range(KD):
                        last = nc.gpsimd.tensor_tensor(
                            decay[v][:, j * P:(j + 1) * P].rearrange("p (h d) -> p h d", d=HD),
                            e_tot[:, j * P:(j + 1) * P].rearrange("p (h d) -> p h d", d=HD),
                            own[:].unsqueeze(2).to_broadcast([P, HB, HD]), ALU.mult)
                    last.then_inc(decay_ready, 1)
                    pool.wait_ge(qkT_taken, f + 1)
                    after(pool, a_ready, 4 * f)
                    for j in range(KD):
                        last = nc.gpsimd.tensor_tensor(
                            qbd[:, j, :, :], qkT[v][:, j, :].unsqueeze(1).to_broadcast([P, HB, P]),
                            own[:].unsqueeze(2).to_broadcast([P, HB, P]), ALU.mult)
                    last.then_inc(qbd_ready, 1)
                    wait_apart(pool, (vn_ready, f + 1), *([] if isinstance(f, int) and f < 1 else [(o_ready, f)]))
                    for j in range(KD):
                        last = nc.gpsimd.tensor_copy(
                            vbd[:, j, :].rearrange("p (h c) -> p h c", c=VSTEP)[:, :, 0:HD],
                            vn[v][:, j * P:(j + 1) * P].rearrange("p (h d) -> p h d", d=HD))
                    last.then_inc(vbd_ready, 1)

            walk(pool, step)

            def tile_step(i, u, ahead, here):
                if here:
                    done = [(m_tok, i + 1), (m_out, i + 1)]
                    if isinstance(i, int) and i == 0:
                        for k in range(2):
                            pool.wait_ge(x1_stored[k], 16 * NC // 2)
                        pool.wait_ge(pads_stored, 16 * (2 * E + 1))
                    else:
                        done.append((added[1 - u], (i + u) * 8))
                    wait_apart(pool, *done)
                    nc.gpsimd.indirect_dma_start(
                        out=out, out_offset=bass.IndirectOffsetOnAxis(ap=tok[u][:, 0:1], axis=0),
                        in_=y_out[u][:], in_offset=None, compute_op=ALU.add,
                    ).then_inc(added[u], 16)

            walk_tiles(pool, tile_step)

        @block.scalar
        def _(act_e):
            A = nc.scalar
            A.preload_act_table_set("natural_log_exp_and_others")
            act_e.wait_ge(small_loaded, 16 * 7)
            A.activation(cnd_e[:], cnd[:], ACT.Exp, scale=-1.0).then_inc(cond_exp, 1)
            order = Order(act_e, act_f)

            def modulate(dst, src, which, sm):
                for j in range(KD):
                    last = A.activation(dst[:, j, :], src[:, j * P:(j + 1) * P], ACT.Identity,
                                        scale=mods[:, which + 2 + j:which + 3 + j], bias=mods[:, which + j:which + j + 1])
                last.then_inc(sm, 1)

            act_e.wait_ge(mods_taken, 1)
            roots = {id(mv_x): Order(act_e, act_x), id(mv_o): Order(act_e, act_o), id(mv_1): Order(act_e, act_1)}

            def inverse_root(mv, n, stats, scale):
                act_e.wait_ge(stats, n + 1)
                roots[id(mv)].begin(n)
                roots[id(mv)].then(A.activation(mv[:, 3:4], mv[:, 1:2], ACT.Ln, bias=eps[:, 0:1]))
                A.activation(mv[:, 2:3], mv[:, 3:4], ACT.Exp, scale=-0.5).then_inc(scale, 1)

            inverse_root(mv_x, 0, x_stats, x_scale)

            def step(c, u, front, back, route):
                f, v = c + 1, 1 - u
                if front:
                    act_e.wait_ge(xT_ready, f + 1)
                    after(act_e, r_ready, f)
                    modulate(hT, p_tr[:, 0:D], 0, hT_ready)
                if route:
                    act_e.wait_ge(x2T_ready, c)
                    after(act_e, score_ready, c - 1)
                    modulate(h2T, p_tr[:, D:2 * D], 4, h2T_ready)
                if front:
                    act_e.wait_ge(proj_ready, f + 1)
                    after(act_e, silu_ready, f)
                    A.activation(eg[:], p_vg[:, D:2 * D], ACT.Exp, scale=-1.0).then_inc(gate_exp, 1)
                    after(act_e, u_ready, f - 1)
                    A.copy(qk[v][:], p_qk[:]).then_inc(qk_taken, 1)
                    act_e.wait_ge(r_ready, f + 1)
                    after(act_e, z_ready, f)
                    A.copy(rT[0:RANK, :], p_z[0:RANK, D:D + P]).then_inc(rT_ready, 1)
                    act_e.wait_ge(z_ready, f + 1)
                    order.begin(f)
                    order.then(A.activation(abs_z[:], p_z[:, 0:D], ACT.Abs))
                    order.then(A.activation(ez[:], abs_z[:], ACT.Exp, scale=-1.0))
                    after(act_e, g_ready, f)
                    A.activation(lz[:], ez[:], ACT.Ln, bias=1.0).then_inc(log1p_ready, 1)
                if back:
                    act_e.wait_ge(o_ready, c + 1)
                    after(act_e, ot_ready, c)
                    A.copy(oT[:], p_o[:, 0:D]).then_inc(oT_taken, 1)
                if route:
                    act_e.wait_ge(gap_ready, c)
                    A.activation(gap_e[:], gap[:], ACT.Exp).then_inc(gap_exp, 1)
                if front:
                    act_e.wait_ge(cum_ready, f + 1)
                    s = 1.0 / GATE_DIVISOR
                    after(act_e, o_ln_ready, f - 1)
                    A.activation(e_pos[v][:], p_cum[:, 0:D], ACT.Exp, scale=s)
                    after(act_e, vn_ready, f)
                    A.activation(e_neg[:], p_cum[:, 0:D], ACT.Exp, scale=-s)
                    after(act_e, decay_ready, f)
                    A.activation(e_tot[:], p_cum[:, D:2 * D], ACT.Exp, scale=s).then_inc(e_ready, 1)
                    act_e.wait_ge(qkT_ready, f + 1)
                    after(act_e, o_ready, f - 1)
                    after(act_e, qbd_ready, f - 1)
                    A.copy(qkT[v][:].rearrange("p a b -> p (a b)"), p_qk[:]).then_inc(qkT_taken, 1)
                if back:
                    inverse_root(mv_o, c, o_stats, o_scale)
                    act_e.wait_ge(owT_ready, c + 1)
                    after(act_e, y_ready, c)
                    A.copy(owT[:], p_a[1][:, 0:D]).then_inc(owT_taken, 1)
                    inverse_root(mv_1, c, x1_stats, x1_scale)
                if front and not (isinstance(c, int) and c + 2 >= NC):
                    inverse_root(mv_x, c + 2, x_stats, x_scale)

            walk(act_e, step)

            def tile_step(i, u, ahead, here):
                if ahead:
                    t = i + 1
                    act_e.wait_ge(m_xT, t + 1)
                    after(act_e, m_hid, t)
                    modulate(xsT, p_tr[:, 0:D], 4, m_xT_taken)
                if here:
                    e = act_e.value_load(tab_e[0:1, bass.ds(i, 1)], min_val=0, max_val=E - 1)
                    act_e.wait_ge(m_hidT, i + 1)
                    after(act_e, m_y, i)
                    for k in range(KF):
                        last = A.activation(act[:, k * P:(k + 1) * P], (p_vg, p_z)[k // 4][:, k % 4 * P:(k % 4 + 1) * P],
                                            ACT.Gelu_apprx_tanh, bias=b1_col[:, bass.ds(e * KF + k, 1)])
                    last.then_inc(m_act, 1)

            act_e.wait_ge(tables_ready, 1)
            walk_tiles(act_e, tile_step)

        @block.vector
        def _(dve):
            V = nc.vector
            setup = Order(dve, dve_s)
            dve.wait_ge(cond_exp, 1)
            setup.then(V.tensor_scalar(cnd_e[:], cnd_e[:], 1.0, None, ALU.add))
            setup.then(V.reciprocal(cnd_e[:], cnd_e[:]))
            setup.then(V.tensor_tensor(cnd_s[:], cnd[:], cnd_e[:], ALU.mult))
            V.tensor_copy(cnd_all[:], cnd_s[:].unsqueeze(2).to_broadcast([P, KD, P])).then_inc(cond_spread, 1)
            dve.wait_ge(mod_ready, 1)
            V.tensor_copy(b1_col[:], p_tr[:, 0:E * KF])
            setup.then(V.tensor_copy(mods[:], p_tr[:, E * KF:E * KF + 8]))
            for at in (2, 6):
                V.tensor_scalar(mods[:, at:at + 2], mods[:, at:at + 2], 1.0, None, ALU.add)
            for dst, src in ((ga, p_qk), (gb, p_vg)):
                setup.then(V.tensor_scalar(tmp_g[:], src[:, 0:D], -1.0, None, ALU.mult))
                setup.then(V.scalar_tensor_tensor(out=dst[:], in0=src[:, 0:D], scalar=MIN_GATE, in1=tmp_g[:],
                                                  op0=ALU.max, op1=ALU.max))
                setup.then(V.tensor_scalar(tmp_g[:], src[:, 0:D], 0.0, 2.0, ALU.is_ge, ALU.mult))
                setup.then(V.scalar_tensor_tensor(out=dst[:], in0=tmp_g[:], scalar=-1.0, in1=dst[:],
                                                  op0=ALU.add, op1=ALU.mult))
            dve.wait_ge(attn_w_loaded, 16 * 9)
            V.tensor_tensor(wout[:], wout[:], ga[:].unsqueeze(1).to_broadcast([P, KD, D]), ALU.mult).then_inc(mods_taken, 1)
            dve.wait_ge(consts_made, 1)

            ln, fo, bo, ro = (Order(dve, s) for s in (dve_ln, dve_f, dve_b, dve_r))

            def norm(o, dst, src, st, mv, n, stats, scale):
                o.then(V.bn_stats(st[:], src), apart=True)
                V.bn_aggr(mv[:, 0:2], st[:]).then_inc(stats, 1)
                dve.wait_ge(scale, n + 1)
                return V.tensor_scalar(dst, src, mv[:, 0:1], mv[:, 2:3], ALU.subtract, ALU.mult)

            def norm_x(n, u):
                ln.begin(n)
                if isinstance(n, int):
                    dve.wait_ge(xin_loaded[u], 16 * (n // 2 + 1))
                else:
                    dve.wait_ge(xin_loaded[u], (n - u) * 8 + 16)
                after(dve, xT_ready, n - 1)
                norm(ln, xn[u][:], x_in[u][:], st_x, mv_x, n, x_stats, x_scale).then_inc(xn_ready, 1)

            norm_x(0, 0)

            def step(c, u, front, back, route):
                f, v = c + 1, 1 - u
                fo.begin(f)
                bo.begin(c)
                ro.begin(c - 1)

                def mask(g):
                    dve.wait_ge(a_ready, 4 * c + g + 1)
                    if g == 0:
                        after(dve, o_ready, c)
                    V.tensor_tensor(am[:, g, :].rearrange("p (h t) -> p h t", t=P),
                                    p_a[g % 2][:].rearrange("p (h t) -> p h t", t=P),
                                    upto[:].unsqueeze(1).to_broadcast([P, 4, P]), ALU.mult).then_inc(am_ready, 1)

                if back:
                    mask(0)
                    mask(1)
                if front:
                    dve.wait_ge(gate_exp, f + 1)
                    after(dve, ln_scales_ready, f)
                    fo.then(V.tensor_scalar(eg[:], eg[:], 1.0, None, ALU.add))
                    fo.then(V.reciprocal(eg[:], eg[:]))
                    V.tensor_tensor(silu[:], p_vg[:, D:2 * D], eg[:], ALU.mult).then_inc(silu_ready, 1)
                if back:
                    mask(2)
                    mask(3)
                if route:
                    dve.wait_ge(score_ready, c)
                    ro.then(V.tensor_tensor(score[:], p_tr[:, 0:E], br_all[:], ALU.add), apart=True)
                    ro.then(V.max(top[:], score[:]), apart=True)
                    ro.then(V.max_index(top_i[:], top[:], score[:]))
                    V.tensor_tensor(gap[:], top[:, 1:2], top[:, 0:1], ALU.subtract).then_inc(gap_ready, 1)
                    ro.then(V.tensor_copy(top_f[:], top_i[:, 0:TOP]))
                    for j in range(TOP):
                        ro.then(V.tensor_scalar(hot[j][:], iota_e[:], top_f[:, j:j + 1], None, ALU.is_equal))
                    V.tensor_tensor(chosen[:], hot[0][:], hot[1][:], ALU.add).then_inc(chosen_ready, 1)
                if front:
                    dve.wait_ge(log1p_ready, f + 1)
                    after(dve, cum_ready, f)
                    V.scalar_tensor_tensor(out=g_log[:], in0=p_z[:, 0:D], scalar=0.0, in1=lz[:], op0=ALU.min,
                                           op1=ALU.subtract).then_inc(g_ready, 1)
                if back:
                    dve.wait_ge(u_ready, c + 1)
                    bo.then(V.tensor_tensor(state_sum[:], p_a[0][:, 0:D], state[:], ALU.add))
                    dve.wait_ge(decay_ready, c + 1)
                    V.tensor_tensor(state[:], state_sum[:], decay[u][:], ALU.mult).then_inc(state_ready, 1)
                    dve.wait_ge(ot_ready, c + 1)
                    bo.then(V.tensor_tensor(o_tok[:], p_o[:, D:2 * D], e_pos[u][:], ALU.mult))
                    bo.then(norm(bo, o_ln[:], o_tok[:], st_o, mv_o, c, o_stats, o_scale))
                    dve.wait_ge(ln_scales_ready, c + 1)
                    bo.then(V.tensor_tensor(o_ln2[:], o_ln[:], w_ln[u][:], ALU.mult))
                    after(dve, owT_ready, c)
                    V.tensor_tensor(o_ln[:], o_ln2[:], b_ln[u][:], ALU.add).then_inc(o_ln_ready, 1)
                if route:
                    dve.wait_ge(rank_ready, c)
                    ro.then(V.tensor_tensor(slot[:], p_tr[:, E:2 * E], base[:], ALU.add))
                    ro.then(V.tensor_tensor(base[:], p_tr[:, 2 * E:3 * E], base[:], ALU.add))
                    for j in range(TOP):
                        ro.then(V.tensor_tensor(pick[:], hot[j][:], slot[:], ALU.mult))
                        ro.then(V.tensor_reduce(pos_f[:, j:j + 1], pick[:], AX_X, ALU.add))
                    if isinstance(c, int):
                        after(dve, rows_sent[v], 16 * TOP * ((c - 1) // 2))
                    else:
                        dve.wait_ge(rows_sent[v], (c - 1 - v) * 16)
                    dve.wait_ge(gap_exp, c)
                    ro.then(V.tensor_scalar(wt[:, 0:1], gap_e[:], 1.0, None, ALU.add))
                    ro.then(V.reciprocal(wt[:, 1:2], wt[:, 0:1]))
                    ro.then(V.tensor_tensor(wt[:, 2:3], gap_e[:], wt[:, 1:2], ALU.mult))
                    ro.then(V.tensor_scalar(wt_a[:], hot[0][:], wt[:, 1:2], None, ALU.mult))
                    ro.then(V.scalar_tensor_tensor(out=rows[v][:, D:D + E], in0=hot[1][:], scalar=wt[:, 2:3],
                                                   in1=wt_a[:], op0=ALU.mult, op1=ALU.add))
                    V.tensor_copy(pos[v][:], pos_f[:]).then_inc(pos_ready, 1)
                if front:
                    dve.wait_ge(e_ready, f + 1)
                    after(dve, u_ready, f - 1)
                    after(dve, vbd_ready, f - 1)
                    V.tensor_tensor(vn[v][:], p_vg[:, 0:D], e_neg[:], ALU.mult).then_inc(vn_ready, 1)
                if back:
                    if isinstance(c, int):
                        dve.wait_ge(xres_loaded[u], 16 * (c // 2 + 1))
                        after(dve, x1_stored[u], 16 * (c // 2))
                        after(dve, rows_sent[u], 16 * TOP * (c // 2))
                    else:
                        dve.wait_ge(xres_loaded[u], (c - u) * 8 + 16)
                        dve.wait_ge(x1_stored[u], (c - u) * 8)
                        dve.wait_ge(rows_sent[u], (c - u) * 16)
                    dve.wait_ge(y_ready, c + 1)
                    V.tensor_tensor(x1[u][:], p_a[1][:, D:2 * D], x_res[u][:], ALU.add).then_inc(x1_ready, 1)
                    dve.wait_ge(x1_ready, c + 1)
                    norm(bo, rows[u][:, 0:D], x1[u][:], st_1, mv_1, c, x1_stats, x1_scale).then_inc(xn2_ready, 1)
                if front and not (isinstance(c, int) and c + 2 >= NC):
                    norm_x(c + 2, u)

            walk(dve, step)

            setup.then(V.tensor_tensor(n_rows[:], base[:], region0[:], ALU.subtract))
            setup.then(V.tensor_tensor(over, n_rows[:].unsqueeze(2).to_broadcast([P, E, NC]),
                                       it32[:].unsqueeze(1).to_broadcast([P, E, NC]), ALU.is_gt))
            setup.then(V.tensor_reduce(n_tiles[:], over, AX_X, ALU.add))
            setup.then(V.tensor_tensor_scan(ends[:], one_e[:], n_tiles[:], 0.0, ALU.mult, ALU.add))
            setup.then(V.tensor_tensor(past, it72[:].unsqueeze(2).to_broadcast([P, TILES, E]),
                                       ends[:].unsqueeze(1).to_broadcast([P, TILES, E]), ALU.is_ge))
            setup.then(V.tensor_reduce(tile_e[:], past, AX_X, ALU.add))
            setup.then(V.tensor_tensor(past_n, past, n_tiles[:].unsqueeze(1).to_broadcast([P, TILES, E]), ALU.mult))
            setup.then(V.tensor_reduce(tile_s[:], past_n, AX_X, ALU.add))
            setup.then(V.tensor_tensor(tile_r[:], it72[:], tile_s[:], ALU.subtract))
            setup.then(V.tensor_scalar(tile_r[:], tile_r[:], float(P), None, ALU.mult))
            setup.then(V.scalar_tensor_tensor(out=tile_r[:], in0=tile_e[:], scalar=float(REGION), in1=tile_r[:],
                                              op0=ALU.mult, op1=ALU.add))
            setup.then(V.tensor_scalar(tile_e[:], tile_e[:], float(E - 1), None, ALU.min))
            V.tensor_copy(tab_e[:], tile_e[:])
            V.tensor_copy(tab_r[:], tile_r[:])
            V.tensor_copy(tab_p[:], base[:]).then_inc(tables_ready, 1)
            dve.wait_ge(tables_ready, 1)

            def tile_step(i, u, ahead, here):
                if ahead:
                    t, v = i + 1, 1 - u
                    dve.wait_ge(m_hid, t + 1)
                    after(dve, m_hidT, t)
                    for k in range(2):
                        last = V.tensor_copy(hid[:, k * 512:(k + 1) * 512], (p_qk, p_cum)[k][:])
                    last.then_inc(m_hid_taken, 1)
                if here:
                    e = dve.value_load(tab_e[0:1, bass.ds(i, 1)], min_val=0, max_val=E - 1)
                    if isinstance(i, int):
                        after(dve, added[u], 16 * (i // 2))
                        if i < 2:
                            for k in range(2):
                                dve.wait_ge(x1_stored[k], 16 * NC // 2)
                        dve.wait_ge(xs_loaded[u], 16 * (i // 2 + 1))
                    else:
                        dve.wait_ge(added[u], (i - u) * 8)
                        dve.wait_ge(xs_loaded[u], (i - u) * 8 + 16)
                    V.tensor_copy(tok[u][:], xs[u][:, ID:ID + 1]).then_inc(m_tok, 1)
                    dve.wait_ge(m_y, i + 1)
                    after(dve, m_out, i)
                    V.tensor_tensor(y_b[:], p_a[u][:, 0:D], b2_all[:, bass.ds(e * D, D)], ALU.add).then_inc(m_y_biased, 1)
                    dve.wait_ge(m_y_biased, i + 1)
                    V.scalar_tensor_tensor(out=y_out[u][:], in0=y_b[:], scalar=xs[u][:, bass.ds(e + D, 1)], in1=gb[:],
                                           op0=ALU.mult, op1=ALU.mult).then_inc(m_out, 1)

            walk_tiles(dve, tile_step)

        @block.tensor
        def _(pe):
            def mm(dst, lhsT, rhs, start, stop):
                return nc.tensor.matmul(dst, lhsT, rhs, start=start, stop=stop, skip_group_check=True)

            pe.wait_ge(small_loaded, 16 * 7)
            pe.wait_ge(consts_made, 1)
            nc.tensor.transpose(p_tr[:, 0:E * KF], b1_rows[:], ident[0:E * KF, 0:E * KF])
            pe.wait_ge(cond_spread, 1)
            for n, part in enumerate((0, 1, 3, 4)):
                for blk in range(KD):
                    for j in range(KD):
                        col = E * KF + 2 * n + blk
                        mm(p_tr[:, col:col + 1], wm[:, j, part * D + blk * P:part * D + (blk + 1) * P],
                           cnd_s[:, j:j + 1], j == 0, j == KD - 1)
            for dst, part in ((p_qk, 2), (p_vg, 5)):
                for j in range(KD):
                    last = mm(dst[:, 0:D], cnd_all[:, j, :], wm[:, j, part * D:(part + 1) * D], j == 0, j == KD - 1)
            last.then_inc(mod_ready, 1)
            pe.wait_ge(mods_taken, 1)

            def step(c, u, front, back, route):
                f, v = c + 1, 1 - u

                def scores_of_heads(g):
                    j = g // 2
                    if g >= 2:
                        pe.wait_ge(am_ready, 4 * c + g - 1)
                    elif g == 0:
                        after(pe, state_ready, c)
                    else:
                        after(pe, x1_ready, c)
                    mm(p_a[g % 2][:], qkT[u][:, KD + j, :],
                       qbd[:, j, 4 * (g % 2):4 * (g % 2) + 4, :].rearrange("p h t -> p (h t)"),
                       True, True).then_inc(a_ready, 1)

                def output_of_block(j):
                    dst = p_o[:, j * P:(j + 1) * P]
                    mm(dst, state[:, j * P:(j + 1) * P], qkT[u][:, j, :], True, False)
                    pe.wait_ge(am_ready, 4 * c + 2 * j + 2)
                    for h in range(HB):
                        last = mm(dst, vbd[:, j, h * P:(h + 1) * P],
                                  am[:, 2 * j + h // 4, h % 4 * P:(h % 4 + 1) * P], False, h == HB - 1)
                    return last

                def transposes(dst, src, n, sm):
                    for k in range(n):
                        last = nc.tensor.transpose(dst[:, k * P:(k + 1) * P], src[:, k * P:(k + 1) * P], ident[:])
                    last.then_inc(sm, 1)

                if front:
                    pe.wait_ge(xn_ready, f + 1)
                    after(pe, pos_ready, c - 1)
                    transposes(p_tr, xn[v], KD, xT_ready)
                if back:
                    pe.wait_ge(qbd_ready, c + 1)
                    scores_of_heads(0)
                    scores_of_heads(1)
                if route:
                    if front:
                        pe.wait_ge(hT_ready, f + 1)
                    pe.wait_ge(xn2_ready, c)
                    transposes(p_tr[:, D:2 * D], rows[v], KD, x2T_ready)
                if front:
                    pe.wait_ge(hT_ready, f + 1)
                    after(pe, qkT_taken, f)
                    after(pe, vn_ready, f)
                    for dst, w in ((p_qk, wqk), (p_vg, wvg)):
                        for j in range(KD):
                            last = mm(dst[:], hT[:, j, :], w[:, j, :], j == 0, j == KD - 1)
                    last.then_inc(proj_ready, 1)
                if back:
                    scores_of_heads(2)
                    scores_of_heads(3)
                if route:
                    pe.wait_ge(h2T_ready, c)
                    for j in range(KD):
                        last = mm(p_tr[:, 0:E], h2T[:, j, :], wr[:, j, :], j == 0, j == KD - 1)
                    last.then_inc(score_ready, 1)
                if front:
                    after(pe, g_ready, f)
                    for j in range(KD):
                        last = mm(p_z[0:RANK, D:D + P], wgk1[:, j, :], hT[:, j, :], j == 0, j == KD - 1)
                    last.then_inc(r_ready, 1)
                if back:
                    after(pe, o_ln_ready, c)
                    after(pe, state_ready, c)
                    pe.wait_ge(vbd_ready, c + 1)
                    output_of_block(0)
                if front:
                    pe.wait_ge(rT_ready, f + 1)
                    mm(p_z[:, 0:D], rT[:], wgk2[:], True, True).then_inc(z_ready, 1)
                if back:
                    output_of_block(1).then_inc(o_ready, 1)
                if route:
                    pe.wait_ge(chosen_ready, c)
                    mm(p_tr[:, E:2 * E], before[:], chosen[:], True, True)
                    mm(p_tr[:, 2 * E:3 * E], ones[:], chosen[:], True, True).then_inc(rank_ready, 1)
                if back:
                    for j in range(KD):
                        last = mm(p_a[0][:, j * P:(j + 1) * P], qk[u][:, D + j * P:D + (j + 1) * P],
                                  vn[u][:, j * P:(j + 1) * P], True, True)
                    last.then_inc(u_ready, 1)
                    pe.wait_ge(oT_taken, c + 1)
                    transposes(p_o[:, D:2 * D], oT, KD, ot_ready)
                if front:
                    pe.wait_ge(g_ready, f + 1)
                    after(pe, e_ready, f)
                    mm(p_cum[:, 0:D], upto[:], g_log[:], True, True)
                    mm(p_cum[:, D:2 * D], ones[:], g_log[:], True, True).then_inc(cum_ready, 1)
                    pe.wait_ge(qk_taken, f + 1)
                    transposes(p_qk, qk[v], 2 * KD, qkT_ready)
                if back:
                    pe.wait_ge(o_ln_ready, c + 1)
                    transposes(p_a[1], o_ln, KD, owT_ready)
                    pe.wait_ge(owT_taken, c + 1)
                    for j in range(KD):
                        last = mm(p_a[1][:, D:2 * D], owT[:, j * P:(j + 1) * P], wout[:, j, :], j == 0, j == KD - 1)
                    last.then_inc(y_ready, 1)

            walk(pe, step)

            pe.wait_ge(experts_loaded, 16 * 2 * E)
            pe.wait_ge(tables_ready, 1)

            def transpose_rows(t, v):
                if isinstance(t, int):
                    pe.wait_ge(xs_loaded[v], 16 * (t // 2 + 1))
                else:
                    pe.wait_ge(xs_loaded[v], (t - v) * 8 + 16)
                after(pe, m_xT_taken, t)
                for k in range(KD):
                    last = nc.tensor.transpose(p_tr[:, k * P:(k + 1) * P], xs[v][:, k * P:(k + 1) * P], ident[:])
                last.then_inc(m_xT, 1)

            def tile_step(i, u, ahead, here):
                if ahead:
                    t, v = i + 1, 1 - u
                    transpose_rows(t, v)
                    e = pe.value_load(tab_e[0:1, bass.ds(t, 1)], min_val=0, max_val=E - 1)
                    pe.wait_ge(m_xT_taken, t + 1)
                    after(pe, m_hid_taken, t)
                    for k, dst in enumerate((p_qk, p_cum)):
                        for j in range(KD):
                            last = mm(dst[:], xsT[:, j, :], w1[:, bass.ds(e * KD * FF + j * FF + k * 512, 512)],
                                      j == 0, j == KD - 1)
                    last.then_inc(m_hid, 1)
                if here:
                    e = pe.value_load(tab_e[0:1, bass.ds(i, 1)], min_val=0, max_val=E - 1)
                    pe.wait_ge(m_act, i + 1)
                    after(pe, m_out, i - 1)
                    for k in range(KF):
                        last = mm(p_a[u][:, 0:D], act[:, k * P:(k + 1) * P], w2[:, bass.ds(e * KF * D + k * D, D)],
                                  k == 0, k == KF - 1)
                    last.then_inc(m_y, 1)
                if ahead:
                    pe.wait_ge(m_hid_taken, t + 1)
                    after(pe, m_act, t)
                    for k in range(KF):
                        last = nc.tensor.transpose((p_vg, p_z)[k // 4][:, k % 4 * P:(k % 4 + 1) * P],
                                                   hid[:, k * P:(k + 1) * P], ident[:])
                    last.then_inc(m_hidT, 1)

            walk_tiles(pe, tile_step)


_INS = ["L0_attn_x", "L0_attn_Wq", "L0_attn_Wk", "L0_attn_Wv", "L0_attn_Wg", "L0_attn_Wgk1", "L0_attn_Wgk2",
        "L0_attn_bgk2", "L0_attn_gamma", "L0_attn_beta", "L0_attn_Wout", "L0_ffn_W1", "L0_ffn_b1", "L0_ffn_W2",
        "L0_ffn_b2", "L0_ffn_Wr", "L0_ffn_br", "L0_c", "L0_wmod"]


def kernel(**inputs):
    import numpy as _np
    import concourse.bacc as _bacc
    from concourse import mybir as _mybir
    from concourse.bass_utils import run_bass_kernel_spmd as _run

    nc = _bacc.Bacc("TRN2", target_bir_lowering=False, num_devices=1)
    arrays, args = {}, []
    for name in _INS:
        a = _np.ascontiguousarray(inputs[name])
        arrays[f"in_{name}_dram"] = a
        args.append(nc.dram_tensor(f"in_{name}_dram", a.shape, _mybir.dt.from_np(a.dtype), kind="ExternalInput").ap())
    _, T, D = inputs["L0_attn_x"].shape
    args.append(nc.dram_tensor("out_0_dram", (T + P, D), _mybir.dt.float32, kind="ExternalOutput").ap())
    build(nc, *args)
    r = _run(nc, [arrays], core_ids=[0])
    return r.results[0]["out_0_dram"][0:T].reshape(1, T, D)
```

```python
from contextlib import ExitStack

import concourse.bass as bass
from concourse import mybir

F32 = mybir.dt.float32
I32 = mybir.dt.int32
U32 = mybir.dt.uint32
ALU = mybir.AluOpType
ACT = mybir.ActivationFunctionType
AX_X = mybir.AxisListType.X

P = 128
EPS = 1e-5
GATE_DIVISOR = 16.0
MIN_GATE = 0.25


def build(nc, x, Wq, Wk, Wv, Wg, Wgk1, Wgk2, bgk2, gamma, beta, Wout, W1, b1, W2, b2, Wr, br, cond, wmod, out):
    _, T, D = x.shape
    E, _, FF = W1.shape
    RANK = Wgk1.shape[1]
    KD = D // P
    KF = FF // P
    HD = 16
    HB = P // HD
    NC = T // P
    TOP = 2
    REGION = T + P
    TILES = TOP * T // P + E
    ROW = D + 16
    ID = D + E
    VSTEP = HB * HD + HD
    assert KD == 2 and NC % 2 == 0 and TILES % 4 == 0 and D == 256

    xt = x.rearrange("b t d -> (b t) d")
    scratch = nc.dram_tensor("expert_rows", (E * REGION + E * P, ROW), F32, kind="Internal").ap()

    with ExitStack() as ctx:
        def sb(name, shape, dt=F32):
            return ctx.enter_context(nc.sbuf_tensor(name, shape, dt))

        def sem(name):
            return ctx.enter_context(nc.semaphore(name))

        def bank(name):
            return ctx.enter_context(nc.psum_tensor(name, [P, 512], F32))

        p_tr = bank("p_tr")
        p_qk = bank("p_qk")
        p_vg = bank("p_vg")
        p_z = bank("p_z")
        p_cum = bank("p_cum")
        p_a = [bank("p_a0"), bank("p_a1")]
        p_o = bank("p_o")

        w1 = sb("w1", [P, E * KD * FF])
        w2 = sb("w2", [P, E * KF * D])
        wqk = sb("wqk", [P, KD, 2 * D])
        wvg = sb("wvg", [P, KD, 2 * D])
        wout = sb("wout", [P, KD, D])
        wgk1 = sb("wgk1", [P, KD, RANK])
        wgk2 = sb("wgk2", [RANK + 1, D])
        wr = sb("wr", [P, KD, E])
        gam = sb("gam", [P, D])
        bet = sb("bet", [P, D])
        br_all = sb("br_all", [P, E])
        b2_all = sb("b2_all", [P, E * D])
        b1_rows = sb("b1_rows", [E * KF, P])
        b1_col = sb("b1_col", [P, E * KF])
        ident = sb("ident", [P, P])
        upto = sb("upto", [P, P])
        before = sb("before", [P, P])
        ones = sb("ones", [P, P])
        own = sb("own", [P, HB])
        eps = sb("eps", [P, 1])
        iota_e = sb("iota_e", [P, E])
        region0 = sb("region0", [P, E])
        ids = sb("ids", [P, NC + 1])
        cnd = sb("cnd", [P, KD])
        cnd_e = sb("cnd_e", [P, KD])
        cnd_s = sb("cnd_s", [P, KD])
        cnd_all = sb("cnd_all", [P, KD, P])
        mods = sb("mods", [P, 8])
        ga = sb("ga", [P, D])
        gb = sb("gb", [P, D])
        tmp_g = sb("tmp_g", [P, D])
        pad_rows = sb("pad_rows", [P, ROW])

        class Lodger:
            def __init__(self, host, start):
                self.host, self.at = host, start

            def take(self, *dims):
                n = 1
                for d in dims:
                    n *= d
                self.at += n
                assert self.at <= self.host.shape[1]
                return self.host[:, self.at - n:self.at]

        LATE = 2
        wm = w2[:, (E - LATE) * KF * D:(E - LATE) * KF * D + KD * 6 * D].rearrange("p (j n) -> p j n", j=KD)
        in_w1, in_w2 = Lodger(w1, (E - LATE) * KD * FF), Lodger(w2, (E - LATE) * KF * D)

        x_in = [sb(f"x_in{i}", [P, D]) for i in range(2)]
        x_res = [sb(f"x_res{i}", [P, D]) for i in range(2)]
        xn = [sb(f"xn{i}", [P, D]) for i in range(2)]
        st_x = sb("st_x", [P, 6])
        mv_x = sb("mv_x", [P, 4])
        hT = sb("hT", [P, KD, P])
        rT = sb("rT", [RANK + 1, P])
        qbd = in_w2.take(KD, HB, P).rearrange("p (a h t) -> p a h t", a=KD, h=HB)
        qk = [in_w2.take(2 * D) for i in range(2)]
        qkT = [sb(f"qkT{i}", [P, 2 * KD, P]) for i in range(2)]
        vbd = in_w1.take(KD, HB * VSTEP).rearrange("p (a c) -> p a c", a=KD)
        vn = [in_w1.take(D) for i in range(2)]
        abs_z = in_w1.take(D)
        ez = in_w1.take(D)
        lz = in_w2.take(D)
        eg = sb("eg", [P, D])
        silu = in_w1.take(D)
        g_log = in_w2.take(D)
        e_pos = [sb(f"e_pos{i}", [P, D]) for i in range(2)]
        e_neg = in_w2.take(D)
        e_tot = in_w2.take(D)
        decay = [in_w1.take(D) for i in range(2)]
        ln_host = sb("ln_host", [P, 4 * ROW])
        w_ln = [ln_host[:, i * D:(i + 1) * D] for i in range(2)]
        b_ln = [ln_host[:, i * D:(i + 1) * D] for i in (2, 3)]
        am = sb("am", [P, 4, 512])
        oT = sb("oT", [P, D])
        o_tok = sb("o_tok", [P, D])
        st_o = sb("st_o", [P, 6])
        mv_o = sb("mv_o", [P, 4])
        o_ln = sb("o_ln", [P, D])
        o_ln2 = sb("o_ln2", [P, D])
        owT = sb("owT", [P, D])
        state = sb("state", [P, D])
        state_sum = sb("state_sum", [P, D])
        x1 = [sb(f"x1{i}", [P, D]) for i in range(2)]
        st_1 = sb("st_1", [P, 6])
        mv_1 = sb("mv_1", [P, 4])
        rows = [sb(f"rows{i}", [P, ROW]) for i in range(2)]
        h2T = sb("h2T", [P, KD, P])
        score = sb("score", [P, E])
        top = sb("top", [P, 8])
        top_i = sb("top_i", [P, 8], U32)
        top_f = sb("top_f", [P, TOP])
        hot = [sb(f"hot{j}", [P, E]) for j in range(TOP)]
        chosen = sb("chosen", [P, E])
        gap = sb("gap", [P, 1])
        gap_e = sb("gap_e", [P, 1])
        wt = sb("wt", [P, 3])
        wt_a = sb("wt_a", [P, E])
        base = sb("base", [P, E])
        slot = sb("slot", [P, E])
        pick = sb("pick", [P, E])
        pos_f = sb("pos_f", [P, TOP])
        pos = [sb(f"pos{i}", [P, TOP], U32) for i in range(2)]

        n_rows = sb("n_rows", [P, E])
        it32 = sb("it32", [P, NC])
        over = am[:, 0, 0:E * NC].rearrange("p (e n) -> p e n", e=E)
        n_tiles = sb("n_tiles", [P, E])
        one_e = sb("one_e", [P, E])
        ends = sb("ends", [P, E])
        it72 = sb("it72", [P, TILES])
        past = am[:, 1:3, :].rearrange("p a b -> p (a b)")[:, 0:TILES * E].rearrange("p (i e) -> p i e", e=E)
        past_n = sb("past_n", [P, TILES, E])[:]
        tile_e = sb("tile_e", [P, TILES])
        tile_s = sb("tile_s", [P, TILES])
        tile_r = sb("tile_r", [P, TILES])
        tab_e = sb("tab_e", [P, TILES], I32)
        tab_r = sb("tab_r", [P, TILES], I32)
        tab_p = sb("tab_p", [P, E], I32)
        xs = [ln_host[:, i * ROW:(i + 1) * ROW] for i in range(4)]
        xsT = h2T
        hid = am[:, 0:2, :].rearrange("p a b -> p (a b)")
        act = am[:, 2:4, :].rearrange("p a b -> p (a b)")
        y_b = o_tok
        y_out = x1
        tok = [sb(f"tok{i}", [P, 1], U32) for i in range(2)]

        small_loaded = sem("small_loaded")
        attn_w_loaded = sem("attn_w_loaded")
        experts_loaded = sem("experts_loaded")
        consts_made = sem("consts_made")
        pool_made = sem("pool_made")
        cond_exp = sem("cond_exp")
        cond_spread = sem("cond_spread")
        mod_ready = sem("mod_ready")
        mods_taken = sem("mods_taken")
        xin_loaded = [sem(f"xin_loaded{i}") for i in range(2)]
        xres_loaded = [sem(f"xres_loaded{i}") for i in range(2)]
        x1_stored = [sem(f"x1_stored{i}") for i in range(2)]
        rows_sent = [sem(f"rows_sent{i}") for i in range(2)]
        dve_ln = sem("dve_ln")
        dve_f = sem("dve_f")
        dve_b = sem("dve_b")
        dve_y = sem("dve_y")
        dve_r = sem("dve_r")
        dve_s = sem("dve_s")
        act_f = sem("act_f")
        act_x = sem("act_x")
        act_o = sem("act_o")
        act_1 = sem("act_1")
        x_stats, x_scale = sem("x_stats"), sem("x_scale")
        o_stats, o_scale = sem("o_stats"), sem("o_scale")
        x1_stats, x1_scale = sem("x1_stats"), sem("x1_scale")
        xn_ready = sem("xn_ready")
        xT_ready = sem("xT_ready")
        hT_ready = sem("hT_ready")
        projqk_ready = sem("projqk_ready")
        proj_ready = sem("proj_ready")
        qk_taken = sem("qk_taken")
        gate_exp = sem("gate_exp")
        silu_ready = sem("silu_ready")
        ln_scales_ready = sem("ln_scales_ready")
        r_ready = sem("r_ready")
        rT_ready = sem("rT_ready")
        z_ready = sem("z_ready")
        log1p_ready = sem("log1p_ready")
        g_ready = sem("g_ready")
        cum_ready = sem("cum_ready")
        e_ready = sem("e_ready")
        decay_ready = sem("decay_ready")
        vn_ready = sem("vn_ready")
        vbd_ready = sem("vbd_ready")
        qkT_ready = sem("qkT_ready")
        qkT_taken = sem("qkT_taken")
        qbd_ready = sem("qbd_ready")
        a_ready = sem("a_ready")
        am_ready = sem("am_ready")
        o_ready = sem("o_ready")
        oT_taken = sem("oT_taken")
        u_ready = sem("u_ready")
        state_ready = sem("state_ready")
        ot_ready = sem("ot_ready")
        o_ln_ready = sem("o_ln_ready")
        owT_ready = sem("owT_ready")
        owT_taken = sem("owT_taken")
        y_ready = sem("y_ready")
        x1_ready = sem("x1_ready")
        xn2_ready = sem("xn2_ready")
        x2T_ready = sem("x2T_ready")
        h2T_ready = sem("h2T_ready")
        score_ready = sem("score_ready")
        gap_ready = sem("gap_ready")
        gap_exp = sem("gap_exp")
        chosen_ready = sem("chosen_ready")
        rank_ready = sem("rank_ready")
        pos_ready = sem("pos_ready")
        id_ready = sem("id_ready")
        pads_stored = sem("pads_stored")
        tables_ready = sem("tables_ready")
        xs_loaded = [sem(f"xs_loaded{i}") for i in range(4)]
        m_xT = sem("m_xT")
        m_xT_taken = sem("m_xT_taken")
        m_hid = sem("m_hid")
        m_hid_taken = sem("m_hid_taken")
        m_hidT = sem("m_hidT")
        m_act = sem("m_act")
        m_y = sem("m_y")
        m_y_biased = sem("m_y_biased")
        m_out = sem("m_out")
        m_tok = sem("m_tok")
        added = [sem(f"added{i}") for i in range(2)]

        block = ctx.enter_context(nc.Block())

        class Order:

            def __init__(self, eng, sm):
                self.eng, self.sm, self.start, self.n, self.per = eng, sm, 0, 0, None

            def begin(self, c):
                if self.n and self.per is None:
                    self.per = self.n
                assert self.n in (0, self.per)
                self.start = 0 if self.per is None else c * self.per
                self.n = 0

            def then(self, ins, apart=False):
                self.n += 1
                ins.then_inc(self.sm, 1)
                if apart:
                    wait_apart(self.eng, (self.sm, self.start + self.n))
                else:
                    self.eng.wait_ge(self.sm, self.start + self.n)

        def wait_apart(eng, *waits):
            waits = [(sm, v if isinstance(v, int) else eng.to_reg(v)) for sm, v in waits]
            eng.wait_ge(consts_made, 1)
            for sm, v in waits:
                eng.wait_ge(sm, v)

        def after(eng, sm, value):
            if not isinstance(value, int) or value > 0:
                eng.wait_ge(sm, value)

        def walk(eng, step):
            step(-1, 1, True, False, False, False)
            step(0, 0, True, True, False, False)
            step(1, 1, True, True, True, False)
            for s in (2, 3):
                step(s, s % 2, True, True, True, True)
            with eng.Fori(2, NC // 2 - 1) as i:
                step(2 * i, 0, True, True, True, True)
                step(2 * i + 1, 1, True, True, True, True)
            step(NC - 2, 0, True, True, True, True)
            step(NC - 1, 1, False, True, True, True)
            step(NC, 0, False, False, True, True)
            step(NC + 1, 1, False, False, False, True)

        def walk_tiles(eng, step):
            step(-2, 2, True, False, False)
            step(-1, 3, True, True, False)
            for i in range(4):
                step(i, i, True, True, True)
            with eng.Fori(1, TILES // 4 - 1) as n:
                for k in range(4):
                    step(4 * n + k, k, True, True, True)
            for i in range(TILES - 4, TILES):
                step(i, i % 4, i + 2 < TILES, i + 1 < TILES, True)

        @block.sync
        def _(sp):
            def load(dst, src, sm):
                sp.dma_start(dst, src).then_inc(sm, 16)

            load(x_in[0][:], xt[0:P, :], xin_loaded[0])
            load(x_in[1][:], xt[P:2 * P, :], xin_loaded[1])
            with nc.allow_non_contiguous_dma(reason="256 numbers"):
                load(cnd[:], cond.rearrange("a (j p) -> p (a j)", p=P), small_loaded)
            load(wm, wmod.rearrange("(j p) n -> p j n", p=P), small_loaded)
            load(gam[:], gamma.rearrange("(a d) -> a d", a=1).to_broadcast([P, D]), small_loaded)
            load(bet[:], beta.rearrange("(a d) -> a d", a=1).to_broadcast([P, D]), small_loaded)
            load(br_all[:], br.rearrange("(a d) -> a d", a=1).to_broadcast([P, E]), small_loaded)
            load(b2_all[:], b2.rearrange("(a e) d -> a (e d)", a=1).to_broadcast([P, E * D]), small_loaded)
            load(b1_rows[:], b1.rearrange("e (j p) -> (e j) p", p=P), small_loaded)
            for k, w in enumerate((Wq, Wk)):
                load(wqk[:, :, k * D:(k + 1) * D], w.rearrange("(j p) n -> p j n", p=P), attn_w_loaded)
            for k, w in enumerate((Wv, Wg)):
                load(wvg[:, :, k * D:(k + 1) * D], w.rearrange("(j p) n -> p j n", p=P), attn_w_loaded)
            load(wout[:], Wout.rearrange("(j p) n -> p j n", p=P), attn_w_loaded)
            load(wgk1[:], Wgk1.rearrange("(j p) n -> p j n", p=P), attn_w_loaded)
            load(wgk2[0:RANK, :], Wgk2, attn_w_loaded)
            load(wgk2[RANK:RANK + 1, :], bgk2.rearrange("(a d) -> a d", a=1), attn_w_loaded)
            load(wr[:], Wr.rearrange("(j p) n -> p j n", p=P), attn_w_loaded)

            sp.wait_ge(consts_made, 1)
            for k in range(E):
                load(scratch[E * REGION + k * P:E * REGION + (k + 1) * P, :], pad_rows[:], pads_stored)
            load(out[T:T + P, :], pad_rows[:, 0:D], pads_stored)

            def expert(e):
                load(w1[:, e * KD * FF:(e + 1) * KD * FF].rearrange("p (j n) -> p j n", j=KD),
                     W1[e].rearrange("(j p) n -> p j n", p=P), experts_loaded)
                load(w2[:, e * KF * D:(e + 1) * KF * D].rearrange("p (j n) -> p j n", j=KF),
                     W2[e].rearrange("(j p) n -> p j n", p=P), experts_loaded)

            def step(s, u, front, back, finish, route):
                v = 1 - u
                if back and not (isinstance(s, int) and s + 2 >= NC):
                    sp.wait_ge(xn_ready, s + 1)
                    load(x_in[u][:], xt[bass.ds((s + 2) * P, P), :], xin_loaded[u])
                if back:
                    after(sp, x1_ready, s - 1)
                    load(x_res[u][:], xt[bass.ds(s * P, P), :], xres_loaded[u])
                if finish:
                    sp.wait_ge(x1_ready, s)
                    load(out[bass.ds((s - 1) * P, P), :], x1[v][:], x1_stored[v])
                if isinstance(s, int) and s == 0:
                    sp.wait_ge(mod_ready, 1)
                    for e in range(E - LATE):
                        expert(e)

            walk(sp, step)

            sp.wait_ge(tables_ready, 1)
            for e in range(E - LATE, E):
                expert(e)

            for e in range(E):
                first = sp.value_load(tab_p[0:1, e:e + 1], min_val=e * REGION, max_val=e * REGION + T)
                load(scratch[bass.ds(first, P), :], pad_rows[:], pads_stored)
            sp.wait_ge(pads_stored, 16 * (2 * E + 1))
            for u in range(2):
                sp.wait_ge(rows_sent[u], 16 * TOP * NC // 2)

            def rows_of(i, slot):
                first = sp.value_load(tab_r[0:1, bass.ds(i, 1)], min_val=0, max_val=E * REGION + (E - 1) * P)
                load(xs[slot][:], scratch[bass.ds(first, P), :], xs_loaded[slot])

            for i in range(3):
                rows_of(i, i)

            def tile_step(i, slot, fetch, ahead, here):
                if here and not (isinstance(i, int) and i + 3 >= TILES):
                    after(sp, m_out, i)
                    rows_of(i + 3, (slot + 3) % 4)

            walk_tiles(sp, tile_step)
            for u in range(2):
                sp.wait_ge(x1_stored[u], 16 * NC // 2)
                sp.wait_ge(added[u], 16 * TILES // 2)

        @block.gpsimd
        def _(pool):
            order = Order(pool, pool_made)
            order.then(nc.gpsimd.memset(ident[:], 0.0))
            order.then(nc.gpsimd.affine_select(out=ident[:], in_=ident[:], compare_op=ALU.not_equal, fill=1.0,
                                               base=0, pattern=[[-1, P]], channel_multiplier=1))
            order.then(nc.gpsimd.memset(ones[:], 1.0))
            nc.gpsimd.affine_select(out=upto[:], in_=ones[:], compare_op=ALU.is_ge, fill=0.0,
                                    base=0, pattern=[[1, P]], channel_multiplier=-1)
            nc.gpsimd.affine_select(out=before[:], in_=ones[:], compare_op=ALU.is_ge, fill=0.0,
                                    base=-1, pattern=[[1, P]], channel_multiplier=-1)
            order.then(nc.gpsimd.affine_select(out=own[:], in_=ones[:, 0:HB], compare_op=ALU.is_ge, fill=0.0,
                                               base=0, pattern=[[-HD, HB]], channel_multiplier=1))
            nc.gpsimd.affine_select(out=own[:], in_=own[:], compare_op=ALU.is_ge, fill=0.0,
                                    base=HD - 1, pattern=[[HD, HB]], channel_multiplier=-1)

            def numbers(dst, pattern, by_partition):
                nc.gpsimd.iota(dst, pattern=pattern, base=0, channel_multiplier=by_partition,
                               allow_small_or_imprecise_dtypes=True)

            numbers(iota_e[:], [[1, E]], 0)
            numbers(region0[:], [[REGION, E]], 0)
            numbers(base[:], [[REGION, E]], 0)
            numbers(ids[:], [[P, NC + 1]], 1)
            numbers(it32[:], [[P, NC]], 0)
            numbers(it72[:], [[1, TILES]], 0)
            order.then(nc.gpsimd.memset(pad_rows[:], 0.0))
            order.then(nc.gpsimd.tensor_copy(pad_rows[:, ID:ID + 1], ids[:, NC:NC + 1]))
            nc.gpsimd.memset(one_e[:], 1.0)
            nc.gpsimd.memset(eps[:], EPS)
            nc.gpsimd.memset(state[:], 0.0)
            for r in rows:
                nc.gpsimd.memset(r[:], 0.0)
            nc.gpsimd.memset(rT[:], 1.0)
            nc.gpsimd.memset(vbd[:], 0.0).then_inc(consts_made, 1)
            pool.wait_ge(consts_made, 1)

            def step(s, u, front, back, finish, route):
                f, v = s + 1, 1 - u
                if front:
                    pool.wait_ge(qkT_taken, f + 1)
                    after(pool, a_ready, 4 * f)
                    for j in range(KD):
                        last = nc.gpsimd.tensor_tensor(
                            qbd[:, j, :, :], qkT[v][:, j, :].unsqueeze(1).to_broadcast([P, HB, P]),
                            own[:].unsqueeze(2).to_broadcast([P, HB, P]), ALU.mult)
                    last.then_inc(qbd_ready, 1)
                    pool.wait_ge(silu_ready, f + 1)
                    after(pool, o_ln_ready, f - 1)
                    nc.gpsimd.tensor_tensor(w_ln[v][:], silu[:], gam[:], ALU.mult)
                    nc.gpsimd.tensor_tensor(b_ln[v][:], silu[:], bet[:], ALU.mult).then_inc(ln_scales_ready, 1)
                if route:
                    r = s - 2
                    wait_apart(pool, (xn2_ready, r + 1))
                    nc.gpsimd.tensor_copy(rows[u][:, ID:ID + 1], ids[:, bass.ds(r, 1)]).then_inc(id_ready, 1)
                    wait_apart(pool, (id_ready, r + 1), (pos_ready, r + 1))
                    for j in range(TOP):
                        nc.gpsimd.indirect_dma_start(
                            out=scratch, out_offset=bass.IndirectOffsetOnAxis(ap=pos[u][:, j:j + 1], axis=0),
                            in_=rows[u][:], in_offset=None,
                        ).then_inc(rows_sent[u], 16)
                if front:
                    pool.wait_ge(e_ready, f + 1)
                    after(pool, state_ready, f - 1)
                    for j in range(KD):
                        last = nc.gpsimd.tensor_tensor(
                            decay[v][:, j * P:(j + 1) * P].rearrange("p (h d) -> p h d", d=HD),
                            e_tot[:, j * P:(j + 1) * P].rearrange("p (h d) -> p h d", d=HD),
                            own[:].unsqueeze(2).to_broadcast([P, HB, HD]), ALU.mult)
                    last.then_inc(decay_ready, 1)
                    wait_apart(pool, (vn_ready, f + 1), *([] if isinstance(f, int) and f < 1 else [(o_ready, f)]))
                    for j in range(KD):
                        last = nc.gpsimd.tensor_copy(
                            vbd[:, j, :].rearrange("p (h c) -> p h c", c=VSTEP)[:, :, 0:HD],
                            vn[v][:, j * P:(j + 1) * P].rearrange("p (h d) -> p h d", d=HD))
                    last.then_inc(vbd_ready, 1)

            walk(pool, step)

            def tile_step(i, slot, fetch, ahead, here):
                u = slot % 2
                if here:
                    done = [(m_tok, i + 1), (m_out, i + 1)]
                    if isinstance(i, int) and i == 0:
                        for k in range(2):
                            pool.wait_ge(x1_stored[k], 16 * NC // 2)
                        pool.wait_ge(pads_stored, 16 * (2 * E + 1))
                    else:
                        done.append((added[1 - u], (i + u) * 8))
                    wait_apart(pool, *done)
                    nc.gpsimd.indirect_dma_start(
                        out=out, out_offset=bass.IndirectOffsetOnAxis(ap=tok[u][:, 0:1], axis=0),
                        in_=y_out[u][:], in_offset=None, compute_op=ALU.add,
                    ).then_inc(added[u], 16)

            walk_tiles(pool, tile_step)

        @block.scalar
        def _(act_e):
            A = nc.scalar
            A.preload_act_table_set("natural_log_exp_and_others")
            act_e.wait_ge(small_loaded, 16 * 7)
            A.activation(cnd_e[:], cnd[:], ACT.Exp, scale=-1.0).then_inc(cond_exp, 1)
            order = Order(act_e, act_f)

            def modulate(dst, src, which, sm):
                for j in range(KD):
                    last = A.activation(dst[:, j, :], src[:, j * P:(j + 1) * P], ACT.Identity,
                                        scale=mods[:, which + 2 + j:which + 3 + j], bias=mods[:, which + j:which + j + 1])
                last.then_inc(sm, 1)

            act_e.wait_ge(mods_taken, 1)
            roots = {id(mv_x): Order(act_e, act_x), id(mv_o): Order(act_e, act_o), id(mv_1): Order(act_e, act_1)}

            def inverse_root(mv, n, stats, scale):
                act_e.wait_ge(stats, n + 1)
                roots[id(mv)].begin(n)
                roots[id(mv)].then(A.activation(mv[:, 3:4], mv[:, 1:2], ACT.Ln, bias=eps[:, 0:1]))
                A.activation(mv[:, 2:3], mv[:, 3:4], ACT.Exp, scale=-0.5).then_inc(scale, 1)

            inverse_root(mv_x, 0, x_stats, x_scale)

            def step(s, u, front, back, finish, route):
                f, v = s + 1, 1 - u
                if front:
                    act_e.wait_ge(xT_ready, f + 1)
                    after(act_e, r_ready, f)
                    modulate(hT, p_tr[:, 0:D], 0, hT_ready)
                if finish:
                    act_e.wait_ge(owT_ready, s)
                    after(act_e, y_ready, s - 1)
                    A.copy(owT[:], p_a[1][:, 0:D]).then_inc(owT_taken, 1)
                if front and not (isinstance(s, int) and s + 2 >= NC):
                    inverse_root(mv_x, s + 2, x_stats, x_scale)
                if front:
                    act_e.wait_ge(projqk_ready, f + 1)
                    after(act_e, u_ready, f - 1)
                    A.copy(qk[v][:], p_qk[:]).then_inc(qk_taken, 1)
                    act_e.wait_ge(proj_ready, f + 1)
                    after(act_e, silu_ready, f)
                    A.activation(eg[:], p_vg[:, D:2 * D], ACT.Exp, scale=-1.0).then_inc(gate_exp, 1)
                if finish:
                    inverse_root(mv_1, s - 1, x1_stats, x1_scale)
                if route:
                    act_e.wait_ge(x2T_ready, s - 1)
                    after(act_e, score_ready, s - 2)
                    modulate(h2T, p_tr[:, D:2 * D], 4, h2T_ready)
                if front:
                    act_e.wait_ge(qkT_ready, f + 1)
                    after(act_e, o_ready, f - 1)
                    after(act_e, qbd_ready, f - 1)
                    A.copy(qkT[v][:].rearrange("p a b -> p (a b)"), p_qk[:]).then_inc(qkT_taken, 1)
                    act_e.wait_ge(r_ready, f + 1)
                    after(act_e, z_ready, f)
                    A.copy(rT[0:RANK, :], p_z[0:RANK, D:D + P]).then_inc(rT_ready, 1)
                if route:
                    act_e.wait_ge(gap_ready, s - 1)
                    A.activation(gap_e[:], gap[:], ACT.Exp).then_inc(gap_exp, 1)
                if front:
                    act_e.wait_ge(z_ready, f + 1)
                    order.begin(f)
                    order.then(A.activation(abs_z[:], p_z[:, 0:D], ACT.Abs))
                    order.then(A.activation(ez[:], abs_z[:], ACT.Exp, scale=-1.0))
                    after(act_e, g_ready, f)
                    A.activation(lz[:], ez[:], ACT.Ln, bias=1.0).then_inc(log1p_ready, 1)
                if back:
                    act_e.wait_ge(o_ready, s + 1)
                    after(act_e, ot_ready, s)
                    A.copy(oT[:], p_o[:, 0:D]).then_inc(oT_taken, 1)
                    inverse_root(mv_o, s, o_stats, o_scale)
                if front:
                    act_e.wait_ge(cum_ready, f + 1)
                    q = 1.0 / GATE_DIVISOR
                    after(act_e, vn_ready, f)
                    A.activation(e_neg[:], p_cum[:, 0:D], ACT.Exp, scale=-q)
                    after(act_e, decay_ready, f)
                    A.activation(e_tot[:], p_cum[:, D:2 * D], ACT.Exp, scale=q)
                    after(act_e, o_ln_ready, f - 1)
                    A.activation(e_pos[v][:], p_cum[:, 0:D], ACT.Exp, scale=q).then_inc(e_ready, 1)

            walk(act_e, step)

            def tile_step(i, slot, fetch, ahead, here):
                if here:
                    e = act_e.value_load(tab_e[0:1, bass.ds(i, 1)], min_val=0, max_val=E - 1)
                    act_e.wait_ge(m_hidT, i + 1)
                    after(act_e, m_y, i)
                    for k in range(KF):
                        last = A.activation(act[:, k * P:(k + 1) * P], (p_vg, p_z)[k // 4][:, k % 4 * P:(k % 4 + 1) * P],
                                            ACT.Gelu_apprx_tanh, bias=b1_col[:, bass.ds(e * KF + k, 1)])
                    last.then_inc(m_act, 1)
                if fetch:
                    t = i + 2
                    act_e.wait_ge(m_xT, t + 1)
                    after(act_e, m_hid, t)
                    modulate(xsT, p_tr[:, 0:D], 4, m_xT_taken)

            act_e.wait_ge(tables_ready, 1)
            walk_tiles(act_e, tile_step)

        @block.vector
        def _(dve):
            V = nc.vector
            setup = Order(dve, dve_s)
            dve.wait_ge(cond_exp, 1)
            setup.then(V.tensor_scalar(cnd_e[:], cnd_e[:], 1.0, None, ALU.add))
            setup.then(V.reciprocal(cnd_e[:], cnd_e[:]))
            setup.then(V.tensor_tensor(cnd_s[:], cnd[:], cnd_e[:], ALU.mult))
            V.tensor_copy(cnd_all[:], cnd_s[:].unsqueeze(2).to_broadcast([P, KD, P])).then_inc(cond_spread, 1)
            dve.wait_ge(mod_ready, 1)
            V.tensor_copy(b1_col[:], p_tr[:, 0:E * KF])
            setup.then(V.tensor_copy(mods[:], p_tr[:, E * KF:E * KF + 8]))
            for at in (2, 6):
                V.tensor_scalar(mods[:, at:at + 2], mods[:, at:at + 2], 1.0, None, ALU.add)
            for dst, src in ((ga, p_qk), (gb, p_vg)):
                setup.then(V.tensor_scalar(tmp_g[:], src[:, 0:D], -1.0, None, ALU.mult))
                setup.then(V.scalar_tensor_tensor(out=dst[:], in0=src[:, 0:D], scalar=MIN_GATE, in1=tmp_g[:],
                                                  op0=ALU.max, op1=ALU.max))
                setup.then(V.tensor_scalar(tmp_g[:], src[:, 0:D], 0.0, 2.0, ALU.is_ge, ALU.mult))
                setup.then(V.scalar_tensor_tensor(out=dst[:], in0=tmp_g[:], scalar=-1.0, in1=dst[:],
                                                  op0=ALU.add, op1=ALU.mult))
            dve.wait_ge(attn_w_loaded, 16 * 9)
            V.tensor_tensor(wout[:], wout[:], ga[:].unsqueeze(1).to_broadcast([P, KD, D]), ALU.mult).then_inc(mods_taken, 1)
            dve.wait_ge(consts_made, 1)

            ln, fo, bo, yo, ro = (Order(dve, s) for s in (dve_ln, dve_f, dve_b, dve_y, dve_r))

            def statistics(o, src, st, mv, stats):
                o.then(V.bn_stats(st[:], src), apart=True)
                V.bn_aggr(mv[:, 0:2], st[:]).then_inc(stats, 1)

            def standardise(dst, src, mv, n, scale):
                dve.wait_ge(scale, n + 1)
                return V.tensor_scalar(dst, src, mv[:, 0:1], mv[:, 2:3], ALU.subtract, ALU.mult)

            def norm_x(n, u):
                ln.begin(n)
                if isinstance(n, int):
                    dve.wait_ge(xin_loaded[u], 16 * (n // 2 + 1))
                else:
                    dve.wait_ge(xin_loaded[u], (n - u) * 8 + 16)
                statistics(ln, x_in[u][:], st_x, mv_x, x_stats)
                after(dve, xT_ready, n - 1)
                standardise(xn[u][:], x_in[u][:], mv_x, n, x_scale).then_inc(xn_ready, 1)

            norm_x(0, 0)

            def step(s, u, front, back, finish, route):
                f, v = s + 1, 1 - u
                fo.begin(f)
                bo.begin(s)
                yo.begin(s - 1)
                ro.begin(s - 2)

                def mask(g):
                    dve.wait_ge(a_ready, 4 * s + g + 1)
                    if g == 0:
                        after(dve, o_ready, s)
                    V.tensor_tensor(am[:, g, :].rearrange("p (h t) -> p h t", t=P),
                                    p_a[g // 2][:].rearrange("p (h t) -> p h t", t=P),
                                    upto[:].unsqueeze(1).to_broadcast([P, 4, P]), ALU.mult).then_inc(am_ready, 1)

                if back:
                    mask(0)
                if front and not (isinstance(s, int) and s + 2 >= NC):
                    norm_x(s + 2, u)
                if back:
                    mask(1)
                if finish:
                    d = s - 1
                    if isinstance(d, int):
                        dve.wait_ge(xres_loaded[v], 16 * (d // 2 + 1))
                        after(dve, x1_stored[v], 16 * (d // 2))
                        after(dve, rows_sent[v], 16 * TOP * (d // 2))
                    else:
                        dve.wait_ge(xres_loaded[v], (d - v) * 8 + 16)
                        dve.wait_ge(x1_stored[v], (d - v) * 8)
                        dve.wait_ge(rows_sent[v], (d - v) * 16)
                    dve.wait_ge(y_ready, d + 1)
                    V.tensor_tensor(x1[v][:], p_a[1][:, D:2 * D], x_res[v][:], ALU.add).then_inc(x1_ready, 1)
                    dve.wait_ge(x1_ready, d + 1)
                    statistics(yo, x1[v][:], st_1, mv_1, x1_stats)
                if back:
                    mask(2)
                if front:
                    dve.wait_ge(gate_exp, f + 1)
                    after(dve, ln_scales_ready, f)
                    fo.then(V.tensor_scalar(eg[:], eg[:], 1.0, None, ALU.add))
                    fo.then(V.reciprocal(eg[:], eg[:]))
                    V.tensor_tensor(silu[:], p_vg[:, D:2 * D], eg[:], ALU.mult).then_inc(silu_ready, 1)
                if finish:
                    standardise(rows[v][:, 0:D], x1[v][:], mv_1, d, x1_scale).then_inc(xn2_ready, 1)
                if back:
                    mask(3)
                if route:
                    r = s - 2
                    dve.wait_ge(score_ready, r + 1)
                    ro.then(V.tensor_tensor(score[:], p_tr[:, 0:E], br_all[:], ALU.add), apart=True)
                    ro.then(V.max(top[:], score[:]), apart=True)
                    ro.then(V.max_index(top_i[:], top[:], score[:]))
                    V.tensor_tensor(gap[:], top[:, 1:2], top[:, 0:1], ALU.subtract).then_inc(gap_ready, 1)
                    ro.then(V.tensor_copy(top_f[:], top_i[:, 0:TOP]))
                    for j in range(TOP):
                        ro.then(V.tensor_scalar(hot[j][:], iota_e[:], top_f[:, j:j + 1], None, ALU.is_equal))
                    V.tensor_tensor(chosen[:], hot[0][:], hot[1][:], ALU.add).then_inc(chosen_ready, 1)
                    dve.wait_ge(gap_exp, r + 1)
                    ro.then(V.tensor_scalar(wt[:, 0:1], gap_e[:], 1.0, None, ALU.add))
                    ro.then(V.reciprocal(wt[:, 1:2], wt[:, 0:1]))
                    ro.then(V.tensor_tensor(wt[:, 2:3], gap_e[:], wt[:, 1:2], ALU.mult))
                    ro.then(V.tensor_scalar(wt_a[:], hot[0][:], wt[:, 1:2], None, ALU.mult))
                    ro.then(V.scalar_tensor_tensor(out=rows[u][:, D:D + E], in0=hot[1][:], scalar=wt[:, 2:3],
                                                   in1=wt_a[:], op0=ALU.mult, op1=ALU.add))
                if front:
                    dve.wait_ge(log1p_ready, f + 1)
                    after(dve, cum_ready, f)
                    V.scalar_tensor_tensor(out=g_log[:], in0=p_z[:, 0:D], scalar=0.0, in1=lz[:], op0=ALU.min,
                                           op1=ALU.subtract).then_inc(g_ready, 1)
                if back:
                    dve.wait_ge(ot_ready, s + 1)
                    bo.then(V.tensor_tensor(o_tok[:], p_o[:, D:2 * D], e_pos[u][:], ALU.mult))
                    statistics(bo, o_tok[:], st_o, mv_o, o_stats)
                    dve.wait_ge(u_ready, s + 1)
                    bo.then(V.tensor_tensor(state_sum[:], p_a[0][:, 0:D], state[:], ALU.add))
                    dve.wait_ge(decay_ready, s + 1)
                    V.tensor_tensor(state[:], state_sum[:], decay[u][:], ALU.mult).then_inc(state_ready, 1)
                    bo.then(standardise(o_ln[:], o_tok[:], mv_o, s, o_scale))
                    dve.wait_ge(ln_scales_ready, s + 1)
                    bo.then(V.tensor_tensor(o_ln2[:], o_ln[:], w_ln[u][:], ALU.mult))
                    after(dve, owT_ready, s)
                    V.tensor_tensor(o_ln[:], o_ln2[:], b_ln[u][:], ALU.add).then_inc(o_ln_ready, 1)
                if front:
                    dve.wait_ge(e_ready, f + 1)
                    after(dve, u_ready, f - 1)
                    after(dve, vbd_ready, f - 1)
                    V.tensor_tensor(vn[v][:], p_vg[:, 0:D], e_neg[:], ALU.mult).then_inc(vn_ready, 1)
                if route:
                    dve.wait_ge(rank_ready, r + 1)
                    ro.then(V.tensor_tensor(slot[:], p_tr[:, E:2 * E], base[:], ALU.add))
                    ro.then(V.tensor_tensor(base[:], p_tr[:, 2 * E:3 * E], base[:], ALU.add))
                    for j in range(TOP):
                        ro.then(V.tensor_tensor(pick[:], hot[j][:], slot[:], ALU.mult))
                        ro.then(V.tensor_reduce(pos_f[:, j:j + 1], pick[:], AX_X, ALU.add))
                    if isinstance(r, int):
                        after(dve, rows_sent[u], 16 * TOP * (r // 2))
                    else:
                        dve.wait_ge(rows_sent[u], (r - u) * 16)
                    V.tensor_copy(pos[u][:], pos_f[:]).then_inc(pos_ready, 1)

            walk(dve, step)

            setup.then(V.tensor_tensor(n_rows[:], base[:], region0[:], ALU.subtract))
            setup.then(V.tensor_tensor(over, n_rows[:].unsqueeze(2).to_broadcast([P, E, NC]),
                                       it32[:].unsqueeze(1).to_broadcast([P, E, NC]), ALU.is_gt))
            setup.then(V.tensor_reduce(n_tiles[:], over, AX_X, ALU.add))
            setup.then(V.tensor_tensor_scan(ends[:], one_e[:], n_tiles[:], 0.0, ALU.mult, ALU.add))
            setup.then(V.tensor_tensor(past, it72[:].unsqueeze(2).to_broadcast([P, TILES, E]),
                                       ends[:].unsqueeze(1).to_broadcast([P, TILES, E]), ALU.is_ge))
            setup.then(V.tensor_reduce(tile_e[:], past, AX_X, ALU.add))
            setup.then(V.tensor_tensor(past_n, past, n_tiles[:].unsqueeze(1).to_broadcast([P, TILES, E]), ALU.mult))
            setup.then(V.tensor_reduce(tile_s[:], past_n, AX_X, ALU.add))
            setup.then(V.tensor_tensor(tile_r[:], it72[:], tile_s[:], ALU.subtract))
            setup.then(V.tensor_scalar(tile_r[:], tile_r[:], float(P), None, ALU.mult))
            setup.then(V.scalar_tensor_tensor(out=tile_r[:], in0=tile_e[:], scalar=float(REGION), in1=tile_r[:],
                                              op0=ALU.mult, op1=ALU.add))
            setup.then(V.tensor_scalar(tile_e[:], tile_e[:], float(E - 1), None, ALU.min))
            V.tensor_copy(tab_e[:], tile_e[:])
            V.tensor_copy(tab_r[:], tile_r[:])
            V.tensor_copy(tab_p[:], base[:]).then_inc(tables_ready, 1)
            dve.wait_ge(tables_ready, 1)

            def tile_step(i, slot, fetch, ahead, here):
                u = slot % 2
                if ahead:
                    t = i + 1
                    dve.wait_ge(m_hid, t + 1)
                    after(dve, m_hidT, t)
                    for k in range(2):
                        last = V.tensor_copy(hid[:, k * 512:(k + 1) * 512], (p_qk, p_cum)[k][:])
                    last.then_inc(m_hid_taken, 1)
                if here:
                    e = dve.value_load(tab_e[0:1, bass.ds(i, 1)], min_val=0, max_val=E - 1)
                    if isinstance(i, int):
                        after(dve, added[u], 16 * (i // 2))
                        if i < 2:
                            for k in range(2):
                                dve.wait_ge(x1_stored[k], 16 * NC // 2)
                        dve.wait_ge(xs_loaded[slot], 16 * (i // 4 + 1))
                    else:
                        dve.wait_ge(added[u], (i - u) * 8)
                        dve.wait_ge(xs_loaded[slot], (i - slot) * 4 + 16)
                    V.tensor_copy(tok[u][:], xs[slot][:, ID:ID + 1]).then_inc(m_tok, 1)
                    dve.wait_ge(m_y, i + 1)
                    after(dve, m_out, i)
                    V.tensor_tensor(y_b[:], p_a[u][:, 0:D], b2_all[:, bass.ds(e * D, D)], ALU.add).then_inc(m_y_biased, 1)
                    dve.wait_ge(m_y_biased, i + 1)
                    V.scalar_tensor_tensor(out=y_out[u][:], in0=y_b[:], scalar=xs[slot][:, bass.ds(e + D, 1)], in1=gb[:],
                                           op0=ALU.mult, op1=ALU.mult).then_inc(m_out, 1)

            walk_tiles(dve, tile_step)

        @block.tensor
        def _(pe):
            def mm(dst, lhsT, rhs, start, stop):
                return nc.tensor.matmul(dst, lhsT, rhs, start=start, stop=stop, skip_group_check=True)

            pe.wait_ge(small_loaded, 16 * 7)
            pe.wait_ge(consts_made, 1)
            nc.tensor.transpose(p_tr[:, 0:E * KF], b1_rows[:], ident[0:E * KF, 0:E * KF])
            pe.wait_ge(cond_spread, 1)
            for n, part in enumerate((0, 1, 3, 4)):
                for blk in range(KD):
                    for j in range(KD):
                        col = E * KF + 2 * n + blk
                        mm(p_tr[:, col:col + 1], wm[:, j, part * D + blk * P:part * D + (blk + 1) * P],
                           cnd_s[:, j:j + 1], j == 0, j == KD - 1)
            for dst, part in ((p_qk, 2), (p_vg, 5)):
                for j in range(KD):
                    last = mm(dst[:, 0:D], cnd_all[:, j, :], wm[:, j, part * D:(part + 1) * D], j == 0, j == KD - 1)
            last.then_inc(mod_ready, 1)
            pe.wait_ge(mods_taken, 1)

            def step(s, u, front, back, finish, route):
                f, v = s + 1, 1 - u

                def scores_of_heads(g):
                    j = g // 2
                    if g == 0:
                        after(pe, state_ready, s)
                    elif g == 2:
                        after(pe, x1_ready, s)
                    else:
                        pe.wait_ge(am_ready, 4 * s + g)
                    mm(p_a[j][:], qkT[u][:, KD + j, :],
                       qbd[:, j, 4 * (g % 2):4 * (g % 2) + 4, :].rearrange("p h t -> p (h t)"),
                       True, True).then_inc(a_ready, 1)

                def output_of_block(j):
                    dst = p_o[:, j * P:(j + 1) * P]
                    mm(dst, state[:, j * P:(j + 1) * P], qkT[u][:, j, :], True, False)
                    pe.wait_ge(am_ready, 4 * s + 2 * j + 2)
                    for h in range(HB):
                        last = mm(dst, vbd[:, j, h * P:(h + 1) * P],
                                  am[:, 2 * j + h // 4, h % 4 * P:(h % 4 + 1) * P], False, h == HB - 1)
                    return last

                def transposes(dst, src, n, sm):
                    for k in range(n):
                        last = nc.tensor.transpose(dst[:, k * P:(k + 1) * P], src[:, k * P:(k + 1) * P], ident[:])
                    last.then_inc(sm, 1)

                def project(dst, w):
                    for j in range(KD):
                        last = mm(dst[:], hT[:, j, :], w[:, j, :], j == 0, j == KD - 1)
                    return last

                if front:
                    pe.wait_ge(xn_ready, f + 1)
                    after(pe, pos_ready, s - 2)
                    transposes(p_tr, xn[v], KD, xT_ready)
                if back:
                    pe.wait_ge(qbd_ready, s + 1)
                    scores_of_heads(0)
                if finish:
                    pe.wait_ge(o_ln_ready, s)
                    pe.wait_ge(am_ready, 4 * s)
                    transposes(p_a[1], o_ln, KD, owT_ready)
                if front:
                    pe.wait_ge(hT_ready, f + 1)
                    after(pe, qkT_taken, f)
                    project(p_qk, wqk).then_inc(projqk_ready, 1)
                if back:
                    scores_of_heads(1)
                if front:
                    after(pe, vn_ready, f)
                    project(p_vg, wvg).then_inc(proj_ready, 1)
                if finish:
                    pe.wait_ge(owT_taken, s)
                    for j in range(KD):
                        last = mm(p_a[1][:, D:2 * D], owT[:, j * P:(j + 1) * P], wout[:, j, :], j == 0, j == KD - 1)
                    last.then_inc(y_ready, 1)
                if route:
                    if front:
                        pe.wait_ge(hT_ready, f + 1)
                    else:
                        pe.wait_ge(pos_ready, s - 2)
                    pe.wait_ge(xn2_ready, s - 1)
                    transposes(p_tr[:, D:2 * D], rows[u], KD, x2T_ready)
                if back:
                    scores_of_heads(2)
                if front:
                    pe.wait_ge(qk_taken, f + 1)
                    transposes(p_qk, qk[v], 2 * KD, qkT_ready)
                if back:
                    scores_of_heads(3)
                if route:
                    pe.wait_ge(h2T_ready, s - 1)
                    for j in range(KD):
                        last = mm(p_tr[:, 0:E], h2T[:, j, :], wr[:, j, :], j == 0, j == KD - 1)
                    last.then_inc(score_ready, 1)
                if front:
                    after(pe, g_ready, f)
                    for j in range(KD):
                        last = mm(p_z[0:RANK, D:D + P], wgk1[:, j, :], hT[:, j, :], j == 0, j == KD - 1)
                    last.then_inc(r_ready, 1)
                if back:
                    after(pe, o_ln_ready, s)
                    after(pe, state_ready, s)
                    pe.wait_ge(vbd_ready, s + 1)
                    output_of_block(0)
                if front:
                    pe.wait_ge(rT_ready, f + 1)
                    mm(p_z[:, 0:D], rT[:], wgk2[:], True, True).then_inc(z_ready, 1)
                if back:
                    output_of_block(1).then_inc(o_ready, 1)
                if route:
                    pe.wait_ge(chosen_ready, s - 1)
                    mm(p_tr[:, E:2 * E], before[:], chosen[:], True, True)
                    mm(p_tr[:, 2 * E:3 * E], ones[:], chosen[:], True, True).then_inc(rank_ready, 1)
                if back:
                    for j in range(KD):
                        last = mm(p_a[0][:, j * P:(j + 1) * P], qk[u][:, D + j * P:D + (j + 1) * P],
                                  vn[u][:, j * P:(j + 1) * P], True, True)
                    last.then_inc(u_ready, 1)
                    pe.wait_ge(oT_taken, s + 1)
                    transposes(p_o[:, D:2 * D], oT, KD, ot_ready)
                if front:
                    pe.wait_ge(g_ready, f + 1)
                    after(pe, e_ready, f)
                    mm(p_cum[:, 0:D], upto[:], g_log[:], True, True)
                    mm(p_cum[:, D:2 * D], ones[:], g_log[:], True, True).then_inc(cum_ready, 1)

            walk(pe, step)

            pe.wait_ge(experts_loaded, 16 * 2 * E)
            pe.wait_ge(tables_ready, 1)

            def tile_step(i, slot, fetch, ahead, here):
                if ahead:
                    t = i + 1
                    e = pe.value_load(tab_e[0:1, bass.ds(t, 1)], min_val=0, max_val=E - 1)
                    pe.wait_ge(m_xT_taken, t + 1)
                    after(pe, m_hid_taken, t)
                    for k, dst in enumerate((p_qk, p_cum)):
                        for j in range(KD):
                            last = mm(dst[:], xsT[:, j, :], w1[:, bass.ds(e * KD * FF + j * FF + k * 512, 512)],
                                      j == 0, j == KD - 1)
                    last.then_inc(m_hid, 1)
                if fetch:
                    n, at = i + 2, (slot + 2) % 4
                    if isinstance(n, int):
                        pe.wait_ge(xs_loaded[at], 16 * (n // 4 + 1))
                    else:
                        pe.wait_ge(xs_loaded[at], (n - at) * 4 + 16)
                    after(pe, m_xT_taken, n)
                    for k in range(KD):
                        last = nc.tensor.transpose(p_tr[:, k * P:(k + 1) * P], xs[at][:, k * P:(k + 1) * P], ident[:])
                    last.then_inc(m_xT, 1)
                if here:
                    e = pe.value_load(tab_e[0:1, bass.ds(i, 1)], min_val=0, max_val=E - 1)
                    pe.wait_ge(m_act, i + 1)
                    after(pe, m_out, i - 1)
                    for k in range(KF):
                        last = mm(p_a[slot % 2][:, 0:D], act[:, k * P:(k + 1) * P], w2[:, bass.ds(e * KF * D + k * D, D)],
                                  k == 0, k == KF - 1)
                    last.then_inc(m_y, 1)
                if ahead:
                    pe.wait_ge(m_hid_taken, t + 1)
                    after(pe, m_act, t)
                    for k in range(KF):
                        last = nc.tensor.transpose((p_vg, p_z)[k // 4][:, k % 4 * P:(k % 4 + 1) * P],
                                                   hid[:, k * P:(k + 1) * P], ident[:])
                    last.then_inc(m_hidT, 1)

            walk_tiles(pe, tile_step)


_INS = ["L0_attn_x", "L0_attn_Wq", "L0_attn_Wk", "L0_attn_Wv", "L0_attn_Wg", "L0_attn_Wgk1", "L0_attn_Wgk2",
        "L0_attn_bgk2", "L0_attn_gamma", "L0_attn_beta", "L0_attn_Wout", "L0_ffn_W1", "L0_ffn_b1", "L0_ffn_W2",
        "L0_ffn_b2", "L0_ffn_Wr", "L0_ffn_br", "L0_c", "L0_wmod"]


def kernel(**inputs):
    import numpy as _np
    import concourse.bacc as _bacc
    from concourse import mybir as _mybir
    from concourse.bass_utils import run_bass_kernel_spmd as _run

    nc = _bacc.Bacc("TRN2", target_bir_lowering=False, num_devices=1)
    arrays, args = {}, []
    for name in _INS:
        a = _np.ascontiguousarray(inputs[name])
        arrays[f"in_{name}_dram"] = a
        args.append(nc.dram_tensor(f"in_{name}_dram", a.shape, _mybir.dt.from_np(a.dtype), kind="ExternalInput").ap())
    _, T, D = inputs["L0_attn_x"].shape
    args.append(nc.dram_tensor("out_0_dram", (T + P, D), _mybir.dt.float32, kind="ExternalOutput").ap())
    build(nc, *args)
    r = _run(nc, [arrays], core_ids=[0])
    return r.results[0]["out_0_dram"][0:T].reshape(1, T, D)
```
